# Optimizing a Trainium2 kernel written in Bass

```python
import numpy as np
import jax
import jax.numpy as jnp

def _softmax(x, axis=-1):
    return jax.nn.softmax(x, axis=axis)

def _gelu(x):
    return jax.nn.gelu(x, approximate=True)

def _silu(x):
    return jax.nn.silu(x)

def _sigmoid(x):
    return jax.nn.sigmoid(x)

def _layernorm(x, axis=-1, eps=1e-05):
    m = jnp.mean(x, axis=axis, keepdims=True)
    v = jnp.var(x, axis=axis, keepdims=True)
    return (x - m) / jnp.sqrt(v + eps)

def _scatter_add(tgt, idx, src, axis=0):
    return tgt.at[idx].add(src)

def _segment_sum(src, seg, n):
    return jax.ops.segment_sum(src, seg, n)
kernel_name = 'mk_seq_preln_d1_jaxref_r4_785af5'

def setup_inputs(seed: int=0):
    np.random.seed(seed)
    _w = jnp.asarray

    def _L0_attn_setup():
        import jax, jax.numpy as jnp
        import numpy as np
        SEQLEN, K, OLDK, HEADS = (512, 256, 256, 16)
        BASE = 10000.0

        def rope(x):
            t = x.shape[1]
            half = K // 2
            theta = 1.0 / BASE ** (jnp.arange(half, dtype=jnp.float32) / half)
            ang = jnp.arange(t, dtype=jnp.float32)[:, None] * theta[None, :]
            cos, sin = (jnp.cos(ang), jnp.sin(ang))
            xr = x.reshape(x.shape[0], t, half, 2)
            xe, xo = (xr[..., 0], xr[..., 1])
            re = xe * cos - xo * sin
            im = xe * sin + xo * cos
            return jnp.stack([re, im], axis=-1).reshape(x.shape)
        key = jax.random.key(seed)
        ks = jax.random.split(key, 5)
        b = 4
        x = jax.random.normal(ks[0], (b, SEQLEN, OLDK), jnp.float32)
        sc_in = 1.0 / np.sqrt(OLDK).astype(np.float32)
        Wq = jax.random.normal(ks[1], (K, OLDK), jnp.float32) * sc_in
        Wk = jax.random.normal(ks[2], (K, OLDK), jnp.float32) * sc_in
        Wv = jax.random.normal(ks[3], (K, OLDK), jnp.float32) * sc_in
        Wu = jax.random.normal(ks[4], (K, K), jnp.float32) * (1.0 / np.sqrt(K).astype(np.float32))
        bu = jnp.zeros((K,), jnp.float32)
        return {'x': x, 'Wq': Wq, 'Wk': Wk, 'Wv': Wv, 'Wu': Wu, 'bu': bu}
    _L0_attn_in = _L0_attn_setup()

    def _L0_ffn_setup():
        import jax, jax.numpy as jnp
        import numpy as np
        DIM = 256

        def _reference_tuple_inner(x, W_r, W_k, W_v, mu_r, mu_k):
            B, T, C = x.shape
            x_prev = jnp.concatenate([jnp.zeros((B, 1, C), x.dtype), x[:, :-1, :]], axis=1)
            xr = mu_r * x + (1.0 - mu_r) * x_prev
            xk = mu_k * x + (1.0 - mu_k) * x_prev
            r = jax.nn.sigmoid(jnp.einsum('btc,dc->btd', xr, W_r))
            k = jnp.einsum('btc,dc->btd', xk, W_k)
            k_act = jnp.square(jax.nn.relu(k))
            out = r * jnp.einsum('btc,dc->btd', k_act, W_v)
            new_state = x[:, -1, :]
            return (out, new_state)
        key = jax.random.key(seed)
        ks = jax.random.split(key, 6)
        B, T, C = (8, 512, DIM)
        x = jax.random.normal(ks[0], (B, T, C), dtype=jnp.float32)
        s = 1.0 / np.sqrt(C)
        W_r = jax.random.uniform(ks[1], (C, C), jnp.float32, -s, s)
        W_k = jax.random.uniform(ks[2], (C, C), jnp.float32, -s, s)
        W_v = jax.random.uniform(ks[3], (C, C), jnp.float32, -s, s)
        mu_r = jax.random.uniform(ks[4], (C,), jnp.float32)
        mu_k = jax.random.uniform(ks[5], (C,), jnp.float32)
        return {'x': x, 'W_r': W_r, 'W_k': W_k, 'W_v': W_v, 'mu_r': mu_r, 'mu_k': mu_k}
    _L0_ffn_in = _L0_ffn_setup()
    _d = {'L0_attn_x': _L0_attn_in['x'], 'L0_attn_Wq': _L0_attn_in['Wq'], 'L0_attn_Wk': _L0_attn_in['Wk'], 'L0_attn_Wv': _L0_attn_in['Wv'], 'L0_attn_Wu': _L0_attn_in['Wu'], 'L0_attn_bu': _L0_attn_in['bu'], 'L0_ffn_W_r': _L0_ffn_in['W_r'], 'L0_ffn_W_k': _L0_ffn_in['W_k'], 'L0_ffn_W_v': _L0_ffn_in['W_v'], 'L0_ffn_mu_r': _L0_ffn_in['mu_r'], 'L0_ffn_mu_k': _L0_ffn_in['mu_k']}
    _x0 = _d['L0_attn_x']
    _d['L0_attn_x'] = jax.random.normal(jax.random.fold_in(jax.random.key(seed), 1), (32, 512, 256), dtype=_x0.dtype)
    del _x0
    return _d

def reference(L0_attn_x, L0_attn_Wq, L0_attn_Wk, L0_attn_Wv, L0_attn_Wu, L0_attn_bu, L0_ffn_W_r, L0_ffn_W_k, L0_ffn_W_v, L0_ffn_mu_r, L0_ffn_mu_k):

    def _L0_attn_ref(x, Wq, Wk, Wv, Wu, bu):
        import jax, jax.numpy as jnp
        import numpy as np
        SEQLEN, K, OLDK, HEADS = (512, 256, 256, 16)
        BASE = 10000.0

        def rope(x):
            t = x.shape[1]
            half = K // 2
            theta = 1.0 / BASE ** (jnp.arange(half, dtype=jnp.float32) / half)
            ang = jnp.arange(t, dtype=jnp.float32)[:, None] * theta[None, :]
            cos, sin = (jnp.cos(ang), jnp.sin(ang))
            xr = x.reshape(x.shape[0], t, half, 2)
            xe, xo = (xr[..., 0], xr[..., 1])
            re = xe * cos - xo * sin
            im = xe * sin + xo * cos
            return jnp.stack([re, im], axis=-1).reshape(x.shape)
        b, t, _ = x.shape
        h = HEADS
        s = K // h
        q = rope(x @ Wq.T)
        k = rope(x @ Wk.T)
        v = x @ Wv.T
        q = q.reshape(b, t, h, s).transpose(0, 2, 1, 3)
        k = k.reshape(b, t, h, s).transpose(0, 2, 1, 3)
        v = v.reshape(b, t, h, s).transpose(0, 2, 1, 3)
        dot = jnp.einsum('bhqd,bhkd->bhqk', q, k) / jnp.sqrt(jnp.float32(s))
        att = jax.nn.softmax(dot, axis=-1)
        out = jnp.einsum('bhqk,bhkd->bhqd', att, v)
        out = out.transpose(0, 2, 1, 3).reshape(b, t, h * s)
        return out @ Wu.T + bu

    def _L0_ffn_ref(x, W_r, W_k, W_v, mu_r, mu_k):
        import jax, jax.numpy as jnp
        import numpy as np
        DIM = 256

        def _reference_tuple_inner(x, W_r, W_k, W_v, mu_r, mu_k):
            B, T, C = x.shape
            x_prev = jnp.concatenate([jnp.zeros((B, 1, C), x.dtype), x[:, :-1, :]], axis=1)
            xr = mu_r * x + (1.0 - mu_r) * x_prev
            xk = mu_k * x + (1.0 - mu_k) * x_prev
            r = jax.nn.sigmoid(jnp.einsum('btc,dc->btd', xr, W_r))
            k = jnp.einsum('btc,dc->btd', xk, W_k)
            k_act = jnp.square(jax.nn.relu(k))
            out = r * jnp.einsum('btc,dc->btd', k_act, W_v)
            new_state = x[:, -1, :]
            return (out, new_state)
        return _reference_tuple_inner(x, W_r, W_k, W_v, mu_r, mu_k)[0]
    x = L0_attn_x
    x = x + _L0_attn_ref(_layernorm(x, axis=-1), L0_attn_Wq, L0_attn_Wk, L0_attn_Wv, L0_attn_Wu, L0_attn_bu)
    x = x + _L0_ffn_ref(_layernorm(x, axis=-1), L0_ffn_W_r, L0_ffn_W_k, L0_ffn_W_v, L0_ffn_mu_r, L0_ffn_mu_k)
    return x

_drawn_inputs = setup_inputs


def setup_inputs(seed=0):
    import zlib

    import numpy as np

    out = dict(_drawn_inputs(seed))
    spreads = {'L0_attn_bu': (0.0, 0.1)}
    factors = {'L0_ffn_W_r': 3.16, 'L0_ffn_mu_r': 6.411}
    for name, (base, spread) in spreads.items():
        noise = np.random.default_rng([zlib.crc32(name.encode()), seed]).standard_normal(out[name].shape)
        drawn = base * np.exp(spread * noise) if base else spread * noise
        out[name] = jnp.asarray(drawn.astype(out[name].dtype))
    for name, factor in factors.items():
        out[name] = (out[name] * factor).astype(out[name].dtype)
    return out
```

```python
from contextlib import ExitStack

import concourse.bass as bass
from concourse import mybir

ALU = mybir.AluOpType
ACT = mybir.ActivationFunctionType
AX = mybir.AxisListType
F32 = mybir.dt.float32
BF16 = mybir.dt.bfloat16

P = 128
B, T, C = 32, 512, 256
H, D = 16, 16
HALF = D // 2
CB = C // P
TC = T // P
GH = 4
NG = H // GH
UNITS = NG * TC
SCORES = UNITS * GH
LEAD = 7
COPIES = 6
SROWS = COPIES * D
MROWS = 3
VW = D + 1
SLOTS = 4
EPS = 1e-5
FIRST, LAST = -3, B + 1
LOOP_FROM, LOOP_PAIRS = 2, 13
CONSTS = 7
LOOP_TO = LOOP_FROM + 2 * LOOP_PAIRS


class Seq:

    def __init__(self, add, i=None):
        self.add, self.i = add, i

    def plus(self, d):
        return Seq(self.add + d, self.i)

    def active(self):
        return self.i is not None or 0 <= self.add < B

    def index(self, eng):
        return self.add if self.i is None else eng.snap(self.i * 2 + self.add)

    def has(self, per, n):
        return self.i is not None or per * self.add + n > 0

    def count(self, per, n):
        if self.i is None:
            return min(max(per * self.add + n, 0), per * B)
        return self.i * (2 * per) + (per * self.add + n)


def layer_kernel(nc, x, wq, wk, wv, wu, bu, w_r, w_k, w_v, mu_r, mu_k, cos_t, sin_t, out):
    scratch = nc.dram_tensor("parts_scratch", [2, 2, 3 * D, H * T], BF16)
    with ExitStack() as ctx:
        def sb(name, shape, dt=F32):
            return ctx.enter_context(nc.sbuf_tensor(name, shape, dt))

        def sem(name):
            return ctx.enter_context(nc.semaphore(name))

        ident = sb("ident", [P, P])
        wT = {n: sb("wT_" + n, [P, CB, C]) for n in ("q", "k", "v", "u", "r", "fk", "fv")}
        cos_sb = sb("cos_sb", [P, T])
        sin_sb = sb("sin_sb", [P, T])
        bu_sb = sb("bu_sb", [P, C])
        mhalf = sb("mhalf", [P, 2])
        mu_sb = sb("mu_sb", [P, 2, CB])
        q_st = [sb(f"q_st{n}", [P, H, T], BF16) for n in range(2)]
        k_st = [sb(f"k_st{n}", [P, H, T], BF16) for n in range(2)]
        v_ext = [sb(f"v_ext{n}", [P, TC, H * VW + 32 - VW]) for n in range(2)]
        probs = sb("probs", [P, SLOTS, GH, T])
        xn = sb("xn", [P, TC, C])
        xnT = sb("xnT", [P, CB, T])
        stats1 = sb("stats1", [P, TC, 6])
        mv1 = sb("mv1", [P, TC, 2])
        rs1 = sb("rs1", [P, TC])
        nm1 = sb("nm1", [P, TC])
        ve1 = sb("ve1", [P, TC])
        mean1 = sb("mean1", [P, TC])
        rope_t = sb("rope_t", [P, 4, T])
        rot = sb("rot", [P, 2, T])
        parts = sb("parts", [P, 2, 3, 2, T], BF16)
        mx = sb("mx", [P, H * TC])
        mres = sb("mres", [GH * TC, P])
        mparts = sb("mparts", [GH * TC, MROWS, P], BF16)
        sums = sb("sums", [P, T])
        inv = sb("inv", [P, T // 32])
        attn = sb("attn", [P, T])
        attnT = sb("attnT", [P, CB, T])
        y = sb("y", [P, TC, C])
        yn = sb("yn", [P, TC, C])
        ynT = sb("ynT", [P, CB, T + 1])
        stats2 = sb("stats2", [P, TC, 6])
        mv2 = sb("mv2", [P, TC, 2])
        rs2 = sb("rs2", [P, TC])
        nm2 = sb("nm2", [P, TC])
        ve2 = sb("ve2", [P, TC])
        mean2 = sb("mean2", [P, TC])
        xrT = sb("xrT", [P, CB, T])
        xkT = sb("xkT", [P, CB, T])
        kT = sb("kT", [P, CB, T])
        gate = sb("gate", [P, TC, C])

        st_ps = ctx.enter_context(nc.psum_tensor("st_ps", [P, 2, T], F32))
        s_ps = ctx.enter_context(nc.psum_tensor("s_ps", [P, 2, T], F32))
        pv_ps = ctx.enter_context(nc.psum_tensor("pv_ps", [P, T], F32))
        mt_ps = ctx.enter_context(nc.psum_tensor("mt_ps", [P, T], F32))
        d_ps = ctx.enter_context(nc.psum_tensor("d_ps", [P, 2, T], F32))

        w_in, c_in, ident_ok, const_ok = sem("w_in"), sem("c_in"), sem("ident_ok"), sem("const_ok")
        wT_ready, wT_done = sem("wT_ready"), sem("wT_done")
        x_in, xres_in, parts_out, stack_in = sem("x_in"), sem("xres_in"), sem("parts_out"), sem("stack_in")
        mrow_in, attn_in, out_stored = sem("mrow_in"), sem("attn_in"), sem("out_stored")
        st_ready, s_ready, pv_done = sem("st_ready"), sem("s_ready"), sem("pv_done")
        xT_ready, qk_ready, v_ready = sem("xT_ready"), sem("qk_ready"), sem("v_ready")
        mt_ready, wu_ready, yT_ready = sem("mt_ready"), sem("wu_ready"), sem("yT_ready")
        k_ready, r_ready, o_ready = sem("k_ready"), sem("r_ready"), sem("o_ready")
        exp_done, xn_done, xnT_done = sem("exp_done"), sem("xn_done"), sem("xnT_done")
        v_done, hi_done, lo_done = sem("v_done"), sem("hi_done"), sem("lo_done")
        yn_done, ynT_done = sem("yn_done"), sem("ynT_done")
        relu_done, tanh_done = sem("relu_done"), sem("tanh_done")
        max_done, msplit = sem("max_done"), sem("msplit")
        ln1_stat, ln2_stat = sem("ln1_stat"), sem("ln2_stat")
        ln1_scale, ln2_scale = sem("ln1_scale"), sem("ln2_scale")
        rope_mul, norm_step, attn_done = sem("rope_mul"), sem("norm_step"), sem("attn_done")
        res_done, gated = sem("res_done"), sem("gated")
        rope_add, sub1, sub2 = sem("rope_add"), sem("sub1"), sem("sub2")
        bu_added, diff_done, shift_done = sem("bu_added"), sem("diff_done"), sem("shift_done")
        ksq_done, out_done = sem("ksq_done"), sem("out_done")

        dve_passed, sp_passed = sem("dve_passed"), sem("sp_passed")

        JOBS = [("V", 1, v_done, 2, 1), ("V", 1, v_done, 2, 2),
                ("XT", 2, xnT_done, 2, 1), ("XT", 2, xnT_done, 2, 2),
                ("WU", -1, res_done, 2, 1), ("WU", -1, res_done, 2, 2),
                ("Q", 2, rope_mul, 8, 2), ("Q", 2, rope_mul, 8, 4),
                ("YT", -1, ynT_done, 2, 1), ("YT", -1, ynT_done, 2, 2),
                ("K", 2, rope_mul, 8, 6), ("K", 2, rope_mul, 8, 8),
                ("FK", -1, relu_done, 2, 1), ("FK", -1, relu_done, 2, 2),
                ("R", -1, tanh_done, 2, 1), ("R", -1, tanh_done, 2, 2),
                ("O", -1, gated, 2, 1), ("O", -1, gated, 2, 2)]
        JOBS_OF = [[0], [1], [2, 3], [4], [5], [6], [7], [8, 9], [10], [11], [12], [13], [14], [15], [16], [17]]

        def bank_reader(b, n):
            while True:
                n -= 2
                if n < 0:
                    n += len(JOBS)
                    b = b.plus(-1)
                if b.i is None and b.add < FIRST:
                    return None
                _, d, done, per, k = JOBS[n]
                if b.plus(d).active():
                    return done, b.plus(d).count(per, k)

        def steps(eng, body):
            for b in range(FIRST, LOOP_FROM):
                body(Seq(b), b % 2)
            with eng.Fori(0, LOOP_PAIRS) as i:
                for par in range(2):
                    body(Seq(LOOP_FROM + par, i), par)
            for b in range(LOOP_TO, LAST + 1):
                body(Seq(b), b % 2)

        def row_max_at(b, u):
            h = u + LEAD
            return (b, h) if h < H else (b.plus(1), h - H)

        block = ctx.enter_context(nc.Block())

        @block.sync
        def _(sp):
            for w, (name, src) in enumerate((("q", wq), ("k", wk), ("v", wv), ("u", wu), ("r", w_r),
                                             ("fk", w_k), ("fv", w_v))):
                sp.dma_start(probs[:, w // GH, w % GH, :].rearrange("p (o c) -> p o c", o=CB),
                             src.rearrange("(o p) c -> p o c", p=P)).then_inc(w_in, 16)
            sp.dma_start(cos_sb[:, :], cos_t).then_inc(c_in, 16)
            sp.dma_start(sin_sb[:, :], sin_t).then_inc(c_in, 16)
            sp.dma_start(bu_sb[:, :], bu.rearrange("(a c) -> a c", a=1).to_broadcast([P, C])).then_inc(c_in, 16)
            for n, mu in enumerate((mu_r, mu_k)):
                for o in range(CB):
                    sp.dma_start(mu_sb[:, n, o:o + 1],
                                 mu[o * P:(o + 1) * P].rearrange("(p a) -> p a", a=1)).then_inc(c_in, 16)

            def carry_wait(b):
                if b.i is not None:
                    sp.sem_inc(sp_passed, 1)

            def step(b, par):
                def store_out():
                    s = b.plus(-2)
                    if s.active():
                        n = s.index(sp)
                        sp.wait_ge(out_done, s.count(2, 2))
                        carry_wait(b)
                        sp.dma_start(out[n].rearrange("(c p) d -> p c d", p=P),
                                     gate[:, :, :]).then_inc(out_stored, 16)

                def load_stacks():
                    s = b.plus(1)
                    if not s.active():
                        return
                    sp.wait_ge(parts_out, s.count(32, 32))
                    carry_wait(b)
                    if b.plus(-1).has(SCORES, SCORES):
                        sp.wait_ge(st_ready, b.plus(-1).count(SCORES, SCORES))
                    n = 1 - par
                    q_src, k_src = scratch[n, 0], scratch[n, 1]
                    row = 0
                    for part, copies in enumerate((3, 2, 1)):
                        rows = q_src[part * D:(part + 1) * D, :]
                        rep = bass.AP(rows.tensor, rows.offset, [[0, copies]] + [list(a) for a in rows.ap])
                        sp.dma_start(q_st[n][row:row + copies * D, :, :].rearrange("p h t -> p (h t)"),
                                     rep).then_inc(stack_in, 16)
                        sp.dma_start(k_st[n][row:row + copies * D, :, :].rearrange("p h t -> p (h t)"),
                                     k_src[0:copies * D, :]).then_inc(stack_in, 16)
                        row += copies * D

                def move_attn(s, g):
                    if not s.active():
                        return
                    sp.wait_ge(attn_done, s.count(4, g + 1))
                    carry_wait(b)
                    if g == 0:
                        if s.plus(-1).has(2, 2):
                            sp.wait_ge(wu_ready, s.plus(-1).count(2, 2))
                    for j in range(GH):
                        row = (g * GH + j) * D
                        sp.dma_start(attnT[row % P:row % P + D, row // P, :],
                                     attn[32 * j:32 * j + D, :]).then_inc(attn_in, 16)

                def move_max(s, g):
                    if not s.active():
                        return
                    sp.wait_ge(msplit, s.count(16, 4 * g + 4))
                    dst = q_st[(s.add) % 2]
                    for m in range(MROWS):
                        sp.dma_start(dst[SROWS + m:SROWS + m + 1, g * GH:(g + 1) * GH, :]
                                     .rearrange("p h (c t) -> p (h c) t", c=TC),
                                     mparts[:, m, :]).then_inc(mrow_in, 16)

                def load_residual():
                    s = b.plus(-1)
                    if s.active():
                        n = s.index(sp)
                        if b.plus(-2).has(2, 2):
                            sp.wait_ge(out_done, b.plus(-2).count(2, 2))
                        carry_wait(b)
                        sp.dma_start(y[:, :, :], x[n].rearrange("(c p) d -> p c d", p=P)).then_inc(xres_in, 16)

                def load_x():
                    s = b.plus(3)
                    if s.active():
                        n = s.index(sp)
                        sp.wait_ge(xT_ready, b.plus(2).count(2, 2))
                        carry_wait(b)
                        sp.dma_start(xn[:, :, :], x[n].rearrange("(c p) d -> p c d", p=P)).then_inc(x_in, 16)

                def store_parts(t):
                    s = b.plus(2)
                    if s.active():
                        sp.wait_ge(sub2, s.count(2, t + 1))
                        carry_wait(b)
                        if b.has(96, 96):
                            sp.wait_ge(stack_in, b.count(96, 96))
                        sp.dma_start(scratch[par, t].rearrange("(k r i) (h c) -> (i h) (k r) c", k=3, r=2, h=H),
                                     parts[:, t, :, :, :].rearrange("p k r c -> p (k r) c")).then_inc(parts_out, 16)

                load_stacks()
                move_attn(b.plus(-1), 3)
                store_out()
                load_residual()
                move_max(b, 1)
                load_x()
                move_attn(b, 0)
                move_max(b, 2)
                move_attn(b, 1)
                move_max(b, 3)
                store_parts(0)
                move_attn(b, 2)
                move_max(b.plus(1), 0)
                store_parts(1)

            steps(sp, step)
            sp.wait_ge(out_stored, 16 * B)

        @block.gpsimd
        def _(pool):
            nc.gpsimd.memset(ident[:, :], 0.0).then_inc(ident_ok, 1)
            pool.wait_ge(ident_ok, 1)
            nc.gpsimd.affine_select(out=ident[:, :], in_=ident[:, :], compare_op=ALU.not_equal, fill=1.0, base=0,
                                    pattern=[[-1, P]], channel_multiplier=1).then_inc(ident_ok, 1)
            pool.wait_ge(ident_ok, 2)
            for n in range(2):
                nc.gpsimd.memset(v_ext[n][:, :, :], 1.0).then_inc(const_ok, 1)
                pool.wait_ge(const_ok, 2 * n + 1)
                nc.gpsimd.memset(k_st[n][SROWS:SROWS + MROWS, :, :], 1.0).then_inc(const_ok, 1)
                pool.wait_ge(const_ok, 2 * n + 2)
            nc.gpsimd.memset(ynT[:, :, 0:1], 0.0).then_inc(const_ok, 1)
            nc.gpsimd.memset(mhalf[:, :], -0.5).then_inc(const_ok, 1)
            pool.wait_ge(const_ok, 6)
            pool.wait_ge(c_in, 16 * CONSTS)

            def step(b, par):
                def finish():
                    s = b.plus(-2)
                    if s.active():
                        for n in range(2):
                            pool.wait_ge(gated, s.count(2, n + 1))
                            t = gate[:, 2 * n:2 * n + 2, :]
                            nc.gpsimd.tensor_tensor(t, t, y[:, 2 * n:2 * n + 2, :], ALU.add).then_inc(out_done, 1)

                def add_bu():
                    s = b.plus(-1)
                    if s.active():
                        pool.wait_ge(xres_in, s.count(16, 16))
                        for c in range(TC):
                            ins = nc.gpsimd.tensor_tensor(y[:, c, :], y[:, c, :], bu_sb[:, :], ALU.add)
                        ins.then_inc(bu_added, 1)

                def rope(t):
                    s = b.plus(2)
                    if s.active():
                        if s.has(2, t):
                            pool.wait_ge(sub2, s.count(2, t))
                        pool.wait_ge(rope_mul, s.count(8, 4 * t + 4))
                        nc.gpsimd.tensor_tensor(rot[:, 0, :], rope_t[:, 0, :], rope_t[:, 1, :],
                                                ALU.subtract).then_inc(rope_add, 1)
                        nc.gpsimd.tensor_tensor(rot[:, 1, :], rope_t[:, 2, :], rope_t[:, 3, :],
                                                ALU.add).then_inc(rope_add, 1)

                def rest1(t):
                    s = b.plus(2)
                    if s.active():
                        pool.wait_ge(hi_done, s.count(2, t + 1))
                        nc.gpsimd.tensor_tensor(rot[:, :, :], rot[:, :, :], parts[:, t, 0, :, :],
                                                ALU.subtract).then_inc(sub1, 1)

                def rest2(t):
                    s = b.plus(2)
                    if s.active():
                        pool.wait_ge(lo_done, s.count(2, t + 1))
                        nc.gpsimd.tensor_tensor(parts[:, t, 2, :, :], rot[:, :, :], parts[:, t, 1, :, :],
                                                ALU.subtract).then_inc(sub2, 1)

                def difference():
                    s = b.plus(-1)
                    if s.active():
                        pool.wait_ge(ynT_done, s.count(2, 2))
                        if s.plus(-1).has(2, 2):
                            pool.wait_ge(r_ready, s.plus(-1).count(2, 2))
                        nc.gpsimd.tensor_tensor(xrT[:, :, :], ynT[:, :, 1:T + 1], ynT[:, :, 0:T],
                                                ALU.subtract).then_inc(diff_done, 1)

                def scales(s, n, stat, scale, ve, mean, rs, nm):
                    if s.active():
                        a, z = 2 * n, 2 * n + 2
                        pool.wait_ge(stat, s.count(6, 3 * n + 3))
                        nc.gpsimd.tensor_tensor(rs[:, a:z], ve[:, a:z], mhalf[:, :], ALU.pow).then_inc(scale, 1)
                        pool.wait_ge(scale, s.count(4, 2 * n + 1))
                        nc.gpsimd.tensor_tensor(nm[:, a:z], mean[:, a:z], rs[:, a:z], ALU.mult).then_inc(scale, 1)

                def square(o):
                    s = b.plus(-1)
                    if s.active():
                        pool.wait_ge(relu_done, s.count(2, o + 1))
                        nc.gpsimd.tensor_tensor(kT[:, o, :], kT[:, o, :], kT[:, o, :], ALU.mult).then_inc(ksq_done, 1)

                finish()
                add_bu()
                for n in range(2):
                    scales(b.plus(-1), n, ln2_stat, ln2_scale, ve2, mean2, rs2, nm2)
                rope(0)
                difference()
                rest1(0)
                rest2(0)
                rope(1)
                scales(b.plus(3), 0, ln1_stat, ln1_scale, ve1, mean1, rs1, nm1)
                rest1(1)
                square(0)
                square(1)
                scales(b.plus(3), 1, ln1_stat, ln1_scale, ve1, mean1, rs1, nm1)
                rest2(1)

            steps(pool, step)

        @block.scalar
        def _(act):
            def step(b, par):
                def v_evac(n):
                    s = b.plus(1)
                    if s.active():
                        act.wait_ge(v_ready, s.count(2, n + 1))
                        if b.plus(-1).has(UNITS, UNITS):
                            act.wait_ge(pv_done, b.plus(-1).count(UNITS, UNITS))
                        nc.scalar.activation(
                            v_ext[1 - par][:, 2 * n:2 * n + 2, 0:H * VW].rearrange("p c (h d) -> p c h d", h=H)[:, :, :, 0:D],
                            d_ps[:, n, :].rearrange("p (c h d) -> p c h d", c=2, h=H), ACT.Copy).then_inc(v_done, 1)

                def xT_evac(n):
                    s = b.plus(2)
                    if s.active():
                        act.wait_ge(xT_ready, s.count(2, n + 1))
                        if s.plus(-1).has(2, 2):
                            act.wait_ge(v_ready, s.plus(-1).count(2, 2))
                        nc.scalar.activation(xnT[:, n, :], d_ps[:, n, :], ACT.Copy).then_inc(xnT_done, 1)

                def yT_evac(n):
                    s = b.plus(-1)
                    if s.active():
                        act.wait_ge(yT_ready, s.count(2, n + 1))
                        if s.plus(-1).has(2, 2):
                            act.wait_ge(shift_done, s.plus(-1).count(2, 2))
                        nc.scalar.activation(ynT[:, n, 1:T + 1], d_ps[:, n, :], ACT.Copy).then_inc(ynT_done, 1)

                def norm1(n):
                    s = b.plus(3)
                    if s.active():
                        act.wait_ge(ln1_scale, s.count(4, 2 * n + 2))
                        for c in (2 * n, 2 * n + 1):
                            nc.scalar.activation(xn[:, c, :], xn[:, c, :], ACT.Identity, scale=rs1[:, c:c + 1],
                                                 bias=nm1[:, c:c + 1]).then_inc(xn_done, 1)

                def norm2(n):
                    s = b.plus(-1)
                    if s.active():
                        act.wait_ge(ln2_scale, s.count(4, 2 * n + 2))
                        if s.plus(-1).has(2, 2):
                            act.wait_ge(yT_ready, s.plus(-1).count(2, 2))
                        for c in (2 * n, 2 * n + 1):
                            nc.scalar.activation(yn[:, c, :], y[:, c, :], ACT.Identity, scale=rs2[:, c:c + 1],
                                                 bias=nm2[:, c:c + 1]).then_inc(yn_done, 1)

                def high(t):
                    s = b.plus(2)
                    if s.active():
                        act.wait_ge(rope_add, s.count(4, 2 * t + 2))
                        if s.plus(-1).has(32, 32):
                            act.wait_ge(parts_out, s.plus(-1).count(32, 32))
                        nc.scalar.activation(parts[:, t, 0, :, :], rot[:, :, :], ACT.Copy).then_inc(hi_done, 1)

                def middle(t):
                    s = b.plus(2)
                    if s.active():
                        act.wait_ge(sub1, s.count(2, t + 1))
                        nc.scalar.activation(parts[:, t, 1, :, :], rot[:, :, :], ACT.Copy).then_inc(lo_done, 1)

                def relu(n):
                    s = b.plus(-1)
                    if s.active():
                        act.wait_ge(k_ready, s.count(2, n + 1))
                        if s.plus(-1).has(2, 2):
                            act.wait_ge(o_ready, s.plus(-1).count(2, 2))
                        nc.scalar.activation(kT[:, n, :], d_ps[:, n, :], ACT.Relu).then_inc(relu_done, 1)

                def tanh(n):
                    s = b.plus(-1)
                    if s.active():
                        act.wait_ge(r_ready, s.count(2, n + 1))
                        if s.has(16, 0):
                            act.wait_ge(out_stored, s.count(16, 0))
                        nc.scalar.activation(gate[:, 2 * n:2 * n + 2, :].rearrange("p c d -> p (c d)"),
                                             d_ps[:, n, :], ACT.Tanh, scale=0.5).then_inc(tanh_done, 1)

                extras = {1: [(v_evac, 0)], 2: [(v_evac, 1)], 3: [(xT_evac, 0), (xT_evac, 1)],
                          5: [(norm2, 0)], 6: [(norm2, 1)], 8: [(yT_evac, 0), (yT_evac, 1)], 9: [(high, 0)],
                          10: [(middle, 0)], 11: [(relu, 0)], 12: [(relu, 1), (high, 1)],
                          13: [(tanh, 0), (middle, 1)], 14: [(tanh, 1), (norm1, 0)], 15: [(norm1, 1)]}
                for u in range(UNITS):
                    for j in range(GH):
                        if b.active():
                            n = GH * u + j
                            act.wait_ge(st_ready, b.count(SCORES, n + 1))
                            if j == 0:
                                if b.has(UNITS, u - SLOTS + 1):
                                    act.wait_ge(pv_done, b.count(UNITS, u - SLOTS + 1))
                            nc.scalar.activation(probs[:, u % SLOTS, j, :], st_ps[:, n % 2, :], ACT.Exp,
                                                 scale=float(D) ** -0.5).then_inc(exp_done, 1)
                        if j % 2 == 1:
                            e = extras.get(u, [])
                            if j == 1 and e:
                                e[0][0](e[0][1])
                            if j == 3 and len(e) > 1:
                                e[1][0](e[1][1])

            steps(act, step)

        @block.vector
        def _(dve):
            for w, name in enumerate(("q", "k", "v", "u", "r", "fk", "fv")):
                dve.wait_ge(wT_ready, w + 1)
                src = d_ps[:, w % 2, :].rearrange("p (o i c) -> p o i c", o=CB, i=CB)
                for o in range(CB):
                    for i in range(CB):
                        if name in ("q", "k"):
                            dst = wT[name][:, i, :].rearrange("p (r i h) -> p r i h", r=2, h=H)[:, :, :, o * 8:o * 8 + 8]
                            ins = nc.vector.tensor_copy(dst, src[:, o, i, :].rearrange("p (h i r) -> p r i h", i=HALF, r=2))
                        elif name == "fv":
                            ins = nc.vector.tensor_scalar(wT[name][:, i, o * P:(o + 1) * P], src[:, o, i, :], 0.5,
                                                          None, ALU.mult)
                        else:
                            ins = nc.vector.tensor_copy(wT[name][:, i, o * P:(o + 1) * P], src[:, o, i, :])
                ins.then_inc(wT_done, 1)
            dve.wait_ge(c_in, 16 * CONSTS)

            def step(b, par):
                def row_max(u, qc):
                    s, h = row_max_at(b, u)
                    if s.active():
                        n = h * TC + qc
                        dve.wait_ge(s_ready, s.count(SCORES, n + 1))
                        nc.vector.tensor_reduce(mx[:, n:n + 1], s_ps[:, n % 2, :], AX.X, ALU.max).then_inc(max_done, 1)

                def split_max(s, g):
                    if not s.active():
                        return
                    m = mt_ps[0:GH * TC, 0:P]
                    dve.wait_ge(mt_ready, s.count(4, g + 1))
                    if s.has(48 * NG, 48 * g):
                        dve.wait_ge(mrow_in, s.count(48 * NG, 48 * g))
                    nc.vector.tensor_scalar(mparts[:, 0, :], m, -1.0, None, ALU.mult).then_inc(msplit, 1)
                    dve.wait_ge(msplit, s.count(16, 4 * g + 1))
                    nc.vector.scalar_tensor_tensor(out=mres[:, :], in0=m, scalar=-1.0, in1=mparts[:, 0, :],
                                                   op0=ALU.mult, op1=ALU.subtract).then_inc(msplit, 1)
                    dve.wait_ge(msplit, s.count(16, 4 * g + 2))
                    nc.vector.tensor_copy(mparts[:, 1, :], mres[:, :]).then_inc(msplit, 1)
                    dve.wait_ge(msplit, s.count(16, 4 * g + 3))
                    nc.vector.tensor_tensor(mparts[:, 2, :], mres[:, :], mparts[:, 1, :], ALU.subtract).then_inc(msplit, 1)

                def normalise(s, g):
                    if not s.active():
                        return
                    dve.wait_ge(pv_done, s.count(UNITS, TC * (g + 1)))
                    nc.vector.transpose(sums[:, :], pv_ps[:, :]).then_inc(norm_step, 1)
                    blocks = sums[:, :].rearrange("p (k r) -> p k r", r=32)
                    dve.wait_ge(norm_step, s.count(3 * NG, 3 * g + 1))
                    nc.vector.reciprocal(inv[:, :], blocks[:, :, D]).then_inc(norm_step, 1)
                    dve.wait_ge(norm_step, s.count(3 * NG, 3 * g + 2))
                    nc.vector.tensor_tensor(blocks[:, :, 0:D], blocks[:, :, 0:D],
                                            inv[:, :].rearrange("p (k r) -> p k r", r=1).to_broadcast([P, T // 32, D]),
                                            ALU.mult).then_inc(norm_step, 1)
                    dve.wait_ge(norm_step, s.count(3 * NG, 3 * g + 3))
                    if s.has(64 * NG, 64 * g):
                        dve.wait_ge(attn_in, s.count(64 * NG, 64 * g))
                    nc.vector.transpose(attn[:, :], sums[:, :]).then_inc(attn_done, 1)

                def residual(n):
                    s = b.plus(-1)
                    if not s.active():
                        return
                    if n == 0:
                        dve.wait_ge(bu_added, s.count(1, 1))
                    dve.wait_ge(wu_ready, s.count(2, n + 1))
                    t = y[:, 2 * n:2 * n + 2, :].rearrange("p c d -> p (c d)")
                    nc.vector.tensor_tensor(t, d_ps[:, n, :], t, ALU.add).then_inc(res_done, 1)
                    dve.wait_ge(res_done, s.count(2, n + 1))
                    layer_stats(s, n, ln2_stat, y, stats2, mv2, ve2, mean2, yn_done)

                def layer_stats(s, n, done, src, stats, mv, ve, nm, used):
                    a, z = 2 * n, 2 * n + 2
                    chunks, per, k = range(a, z), 6, 3 * n
                    for c in chunks:
                        ins = nc.vector.bn_stats(stats[:, c, :], src[:, c, :])
                    ins.then_inc(done, 1)
                    dve.wait_ge(done, s.count(per, k + 1))
                    dve.sem_inc(dve_passed, 1)
                    for c in chunks:
                        ins = nc.vector.bn_aggr(mv[:, c, :], stats[:, c, :])
                    ins.then_inc(done, 1)
                    dve.wait_ge(done, s.count(per, k + 2))
                    if s.plus(-1).has(4, 4):
                        dve.wait_ge(used, s.plus(-1).count(4, 4))
                    nc.vector.tensor_scalar(ve[:, a:z], mv[:, a:z, 1], EPS, None, ALU.add)
                    nc.vector.tensor_scalar(nm[:, a:z], mv[:, a:z, 0], -1.0, None, ALU.mult).then_inc(done, 1)

                def stats1_of(n):
                    s = b.plus(3)
                    if s.active():
                        dve.wait_ge(x_in, s.count(16, 16))
                        layer_stats(s, n, ln1_stat, xn, stats1, mv1, ve1, mean1, xn_done)

                def rope_mults(n):
                    s = b.plus(2)
                    if s.active():
                        dve.wait_ge(qk_ready, s.count(4, n + 1))
                        if n == 0:
                            if s.plus(-1).has(4, 4):
                                dve.wait_ge(rope_add, s.plus(-1).count(4, 4))
                        if n == 2:
                            dve.wait_ge(rope_add, s.count(4, 2))
                        for slot, table in (((0, cos_sb), (2, sin_sb)), ((1, sin_sb), (3, cos_sb)))[n % 2]:
                            nc.vector.tensor_tensor(rope_t[:, slot, :], d_ps[:, n % 2, :], table[:, :],
                                                    ALU.mult).then_inc(rope_mul, 1)

                def shift(n, dst):
                    s = b.plus(-1)
                    if not s.active():
                        return
                    if n == 1:
                        dve.wait_ge(diff_done, s.count(1, 1))
                        if s.plus(-1).has(2, 2):
                            dve.wait_ge(k_ready, s.plus(-1).count(2, 2))
                    for o in range(CB):
                        ins = nc.vector.scalar_tensor_tensor(out=dst[:, o, :], in0=xrT[:, o, :], in1=ynT[:, o, 0:T],
                                                             scalar=mu_sb[:, n, o:o + 1], op0=ALU.mult, op1=ALU.add)
                    ins.then_inc(shift_done, 1)

                def gate_v(s, n):
                    if s.active():
                        dve.wait_ge(o_ready, s.count(2, n + 1))
                        dve.wait_ge(tanh_done, s.count(2, n + 1))
                        t = gate[:, 2 * n:2 * n + 2, :].rearrange("p c d -> p (c d)")
                        nc.vector.scalar_tensor_tensor(out=t, in0=t, scalar=1.0, in1=d_ps[:, n, :],
                                                       op0=ALU.add, op1=ALU.mult).then_inc(gated, 1)

                prev, nxt = b.plus(-1), b.plus(1)
                extras = {(0, 0): [(gate_v, b.plus(-2), 1)], (0, 3): [(normalise, prev, 3)],
                          (2, 0): [(split_max, b, 1)], (4, 1): [(residual, 0)], (4, 3): [(normalise, b, 0)],
                          (5, 1): [(residual, 1)], (6, 0): [(split_max, b, 2)], (6, 2): [(rope_mults, 0)],
                          (7, 1): [(rope_mults, 1)], (8, 3): [(normalise, b, 1)], (9, 1): [(rope_mults, 2)], (9, 3): [(shift, 1, xkT)],
                          (10, 0): [(split_max, b, 3)], (10, 2): [(rope_mults, 3)], (11, 1): [(stats1_of, 0)], (11, 3): [(shift, 0, xrT)],
                          (12, 1): [(stats1_of, 1)], (12, 3): [(normalise, b, 2)],
                          (14, 0): [(split_max, nxt, 0)], (15, 1): [(gate_v, prev, 0)]}
                for u in range(UNITS):
                    for qc in range(TC):
                        row_max(u, qc)
                        for f, *args in extras.get((u, qc), []):
                            f(*args)

            steps(dve, step)

        @block.tensor
        def _(pe):
            pe.wait_ge(ident_ok, 2)
            pe.wait_ge(w_in, 16 * 7)
            for w in range(7):
                if w >= 2:
                    pe.wait_ge(wT_done, w - 1)
                src = probs[:, w // GH, w % GH, :].rearrange("p (o c) -> p o c", o=CB)
                for o in range(CB):
                    for i in range(CB):
                        ins = nc.tensor.transpose(d_ps[:, w % 2, (o * CB + i) * P:(o * CB + i + 1) * P],
                                                  src[:, o, i * P:(i + 1) * P], ident[:, :])
                ins.then_inc(wT_ready, 1)
            pe.wait_ge(wT_done, 7)
            pe.wait_ge(const_ok, 6)

            def step(b, par):
                def score_T(u, j):
                    if not b.active():
                        return
                    g, c = divmod(u, TC)
                    n, h = GH * u + j, GH * g + j
                    if c == 0 and j == 0:
                        pe.wait_ge(mrow_in, b.count(48 * NG, 48 * (g + 1)))
                    if b.has(SCORES, n - 1):
                        pe.wait_ge(exp_done, b.count(SCORES, n - 1))
                    nc.tensor.matmul(st_ps[:, n % 2, :], k_st[par][0:SROWS + MROWS, h, c * P:(c + 1) * P],
                                     q_st[par][0:SROWS + MROWS, h, :], start=True, stop=True).then_inc(st_ready, 1)

                def score(u, qc):
                    s, h = row_max_at(b, u)
                    if not s.active():
                        return
                    n, half = h * TC + qc, s.add % 2
                    if n == 0:
                        pe.wait_ge(stack_in, s.count(96, 96))
                    if s.has(SCORES, n - 1):
                        pe.wait_ge(max_done, s.count(SCORES, n - 1))
                    nc.tensor.matmul(s_ps[:, n % 2, :], q_st[half][0:SROWS, h, qc * P:(qc + 1) * P],
                                     k_st[half][0:SROWS, h, :], start=True, stop=True).then_inc(s_ready, 1)

                def values(s, half, u):
                    if not s.active():
                        return
                    g, c = divmod(u, TC)
                    pe.wait_ge(exp_done, s.count(SCORES, GH * (u + 1)))
                    if u == 0:
                        pe.wait_ge(v_done, s.count(2, 2))
                    if c == 0:
                        if s.has(NG, g):
                            pe.wait_ge(attn_done, s.count(NG, g))
                    for j in range(GH):
                        h = GH * g + j
                        ins = nc.tensor.matmul(pv_ps[32 * j:32 * j + 32, :], v_ext[half][:, c, VW * h:VW * h + 32],
                                               probs[:, u % SLOTS, j, :], start=(c == 0), stop=(c == TC - 1))
                    ins.then_inc(pv_done, 1)

                def row_max_T(s, g):
                    if not s.active():
                        return
                    pe.wait_ge(max_done, s.count(SCORES, GH * TC * (g + 1)))
                    if s.has(16, 4 * g):
                        pe.wait_ge(msplit, s.count(16, 4 * g))
                    w = GH * TC
                    nc.tensor.transpose(mt_ps[0:w, 0:P], mx[:, g * w:(g + 1) * w], ident[:, :]).then_inc(mt_ready, 1)

                def dense(u):
                    for job in JOBS_OF[u]:
                        name, d, _, _, k = JOBS[job]
                        s, n, half = b.plus(d), job % 2, job % 2
                        if not s.active():
                            continue
                        free = bank_reader(b, job)
                        if free is not None:
                            pe.wait_ge(free[0], free[1])
                        bank = d_ps[:, half, :]
                        if name == "XT":
                            pe.wait_ge(xn_done, s.count(4, 4))
                            for c in range(TC):
                                ins = nc.tensor.transpose(bank[:, c * P:(c + 1) * P], xn[:, c, n * P:(n + 1) * P], ident[:, :])
                            ins.then_inc(xT_ready, 1)
                        elif name == "YT":
                            pe.wait_ge(yn_done, s.count(4, 4))
                            for c in range(TC):
                                ins = nc.tensor.transpose(bank[:, c * P:(c + 1) * P], yn[:, c, n * P:(n + 1) * P], ident[:, :])
                            ins.then_inc(yT_ready, 1)
                        elif name in ("Q", "K", "FK"):
                            if name == "FK":
                                pe.wait_ge(shift_done, s.count(2, 1))
                                w, src, done = wT["fk"], xkT, k_ready
                            else:
                                pe.wait_ge(xnT_done, s.count(2, 2))
                                w, src, done = wT[name.lower()], xnT, qk_ready
                            for i in range(CB):
                                ins = nc.tensor.matmul(bank, w[:, i, n * P:(n + 1) * P], src[:, i, :],
                                                       start=(i == 0), stop=(i == CB - 1))
                            ins.then_inc(done, 1)
                        else:
                            w, src, done = {"V": (wT["v"], xnT, v_ready), "WU": (wT["u"], attnT, wu_ready),
                                            "R": (wT["r"], xrT, r_ready), "O": (wT["fv"], kT, o_ready)}[name]
                            if name == "WU":
                                pe.wait_ge(attn_in, s.count(64 * NG, 64 * NG))
                            if name == "R":
                                pe.wait_ge(shift_done, s.count(2, 2))
                            if name == "O":
                                pe.wait_ge(ksq_done, s.count(2, 2))
                            for m in range(2):
                                c = 2 * n + m
                                for i in range(CB):
                                    ins = nc.tensor.matmul(bank[:, m * C:(m + 1) * C], src[:, i, c * P:(c + 1) * P],
                                                           w[:, i, :], start=(i == 0), stop=(i == CB - 1))
                            ins.then_inc(done, 1)

                for u in range(UNITS):
                    for j in range(2):
                        score_T(u, j)
                        score(u, j)
                    if u == 0:
                        values(b.plus(-1), 1 - par, UNITS - 1)
                    else:
                        values(b, par, u - 1)
                    for j in range(2, GH):
                        score_T(u, j)
                        score(u, j)
                    dense(u)
                    if u in (1, 5, 9):
                        row_max_T(b, (u + 3) // 4)
                    if u == 13:
                        row_max_T(b.plus(1), 0)

            steps(pe, step)


_INS = ["L0_attn_x", "L0_attn_Wq", "L0_attn_Wk", "L0_attn_Wv", "L0_attn_Wu", "L0_attn_bu",
        "L0_ffn_W_r", "L0_ffn_W_k", "L0_ffn_W_v", "L0_ffn_mu_r", "L0_ffn_mu_k"]


def kernel(**inputs):
    import numpy as np
    import concourse.bacc as bacc
    from concourse.bass_utils import run_bass_kernel_spmd

    half = C // 2
    theta = (np.float32(1.0) / np.float32(10000.0) ** (np.arange(half, dtype=np.float32) / np.float32(half))).astype(np.float32)
    angle = np.arange(T, dtype=np.float32)[None, :] * theta[:, None]
    order = np.arange(half).reshape(H, HALF).T.reshape(-1)
    tables = {"cos": np.cos(angle)[order].astype(np.float32), "sin": np.sin(angle)[order].astype(np.float32)}

    nc = bacc.Bacc("TRN2", target_bir_lowering=False, num_devices=1)
    arrays, args = {}, []
    for name, a in [(n, inputs[n]) for n in _INS] + list(tables.items()):
        a = np.ascontiguousarray(a)
        arrays[f"in_{name}_dram"] = a
        args.append(nc.dram_tensor(f"in_{name}_dram", a.shape, mybir.dt.from_np(a.dtype), kind="ExternalInput").ap())
    args.append(nc.dram_tensor("out_0_dram", (B, T, C), F32, kind="ExternalOutput").ap())
    layer_kernel(nc, *args)
    r = run_bass_kernel_spmd(nc, [arrays], core_ids=[0])
    return r.results[0]["out_0_dram"]
```

```python
from contextlib import ExitStack

import concourse.bass as bass
from concourse import mybir

ALU = mybir.AluOpType
ACT = mybir.ActivationFunctionType
AX = mybir.AxisListType
F32 = mybir.dt.float32
BF16 = mybir.dt.bfloat16

P = 128
B, T, C = 32, 512, 256
H, D = 16, 16
HALF = D // 2
CB = C // P
TC = T // P
GH = 4
NG = H // GH
UNITS = NG * TC
SCORES = UNITS * GH
LEAD = 7
COPIES = 6
SROWS = COPIES * D
MROWS = 3
VW = D + 1
SLOTS = 4
EPS = 1e-5
FIRST, LAST = -3, B + 1
LOOP_FROM, LOOP_PAIRS = 2, 13
CONSTS = 7
LOOP_TO = LOOP_FROM + 2 * LOOP_PAIRS


class Seq:

    def __init__(self, add, i=None):
        self.add, self.i = add, i

    def plus(self, d):
        return Seq(self.add + d, self.i)

    def active(self):
        return self.i is not None or 0 <= self.add < B

    def index(self, eng):
        return self.add if self.i is None else eng.snap(self.i * 2 + self.add)

    def has(self, per, n):
        return self.i is not None or per * self.add + n > 0

    def count(self, per, n):
        if self.i is None:
            return min(max(per * self.add + n, 0), per * B)
        return self.i * (2 * per) + (per * self.add + n)


def layer_kernel(nc, x, wq, wk, wv, wu, bu, w_r, w_k, w_v, mu_r, mu_k, cos_t, sin_t, out):
    scratch = nc.dram_tensor("parts_scratch", [2, 2, 3 * D, H * T], BF16)
    with ExitStack() as ctx:
        def sb(name, shape, dt=F32):
            return ctx.enter_context(nc.sbuf_tensor(name, shape, dt))

        def sem(name):
            return ctx.enter_context(nc.semaphore(name))

        ident = sb("ident", [P, P])
        wT = {n: sb("wT_" + n, [P, CB, C]) for n in ("q", "k", "v", "u", "r", "fk", "fv")}
        cos_sb = sb("cos_sb", [P, T])
        sin_sb = sb("sin_sb", [P, T])
        bu_sb = sb("bu_sb", [P, C])
        mhalf = sb("mhalf", [P, 2])
        mu_sb = sb("mu_sb", [P, 2, CB])
        q_st = [sb(f"q_st{n}", [P, H, T], BF16) for n in range(2)]
        k_st = [sb(f"k_st{n}", [P, H, T], BF16) for n in range(2)]
        v_ext = [sb(f"v_ext{n}", [P, TC, H * VW + 32 - VW]) for n in range(2)]
        probs = sb("probs", [P, SLOTS, GH, T])
        xn = sb("xn", [P, TC, C])
        xnT = sb("xnT", [P, CB, T])
        stats1 = sb("stats1", [P, TC, 6])
        mv1 = sb("mv1", [P, TC, 2])
        rs1 = sb("rs1", [P, TC])
        nm1 = sb("nm1", [P, TC])
        ve1 = sb("ve1", [P, TC])
        mean1 = sb("mean1", [P, TC])
        rope_t = sb("rope_t", [P, 4, T])
        rot = sb("rot", [P, 2, T])
        parts = sb("parts", [P, 2, 3, 2, T], BF16)
        mx = sb("mx", [P, H * TC])
        mres = sb("mres", [GH * TC, P])
        mparts = sb("mparts", [GH * TC, MROWS, P], BF16)
        sums = sb("sums", [P, T])
        inv = sb("inv", [P, T // 32])
        attn = sb("attn", [P, T])
        attnT = sb("attnT", [P, CB, T])
        y = sb("y", [P, TC, C])
        yn = sb("yn", [P, TC, C])
        ynT = sb("ynT", [P, CB, T + 1])
        stats2 = sb("stats2", [P, TC, 6])
        mv2 = sb("mv2", [P, TC, 2])
        rs2 = sb("rs2", [P, TC])
        nm2 = sb("nm2", [P, TC])
        ve2 = sb("ve2", [P, TC])
        mean2 = sb("mean2", [P, TC])
        xrT = sb("xrT", [P, CB, T])
        xkT = sb("xkT", [P, CB, T])
        kT = sb("kT", [P, CB, T])
        gate = sb("gate", [P, TC, C])

        st_ps = ctx.enter_context(nc.psum_tensor("st_ps", [P, 2, T], F32))
        s_ps = ctx.enter_context(nc.psum_tensor("s_ps", [P, 2, T], F32))
        pv_ps = ctx.enter_context(nc.psum_tensor("pv_ps", [P, 2, T], F32))
        d_ps = ctx.enter_context(nc.psum_tensor("d_ps", [P, 2, T], F32))

        w_in, c_in, ident_ok, const_ok = sem("w_in"), sem("c_in"), sem("ident_ok"), sem("const_ok")
        wT_ready, wT_done = sem("wT_ready"), sem("wT_done")
        x_in, xres_in, parts_out, stack_in = sem("x_in"), sem("xres_in"), sem("parts_out"), sem("stack_in")
        mrow_in, attn_in, out_stored = sem("mrow_in"), sem("attn_in"), sem("out_stored")
        st_ready, s_ready, pv_done = sem("st_ready"), sem("s_ready"), sem("pv_done")
        xT_ready, qk_ready, v_ready = sem("xT_ready"), sem("qk_ready"), sem("v_ready")
        mt_ready, wu_ready, yT_ready = sem("mt_ready"), sem("wu_ready"), sem("yT_ready")
        k_ready, r_ready, o_ready = sem("k_ready"), sem("r_ready"), sem("o_ready")
        exp_done, xn_done, xnT_done = sem("exp_done"), sem("xn_done"), sem("xnT_done")
        v_done, hi_done, lo_done = sem("v_done"), sem("hi_done"), sem("lo_done")
        yn_done, ynT_done = sem("yn_done"), sem("ynT_done")
        relu_done, tanh_done = sem("relu_done"), sem("tanh_done")
        max_done, msplit = sem("max_done"), sem("msplit")
        ln1_stat, ln2_stat = sem("ln1_stat"), sem("ln2_stat")
        ln1_scale, ln2_scale = sem("ln1_scale"), sem("ln2_scale")
        norm_step, attn_done = sem("norm_step"), sem("attn_done")
        res_done, gated = sem("res_done"), sem("gated")
        qk_done, rope_step = sem("qk_done"), sem("rope_step")
        sub1, sub2 = sem("sub1"), sem("sub2")
        bu_added, diff_done, shift_done = sem("bu_added"), sem("diff_done"), sem("shift_done")
        ksq_done, out_done = sem("ksq_done"), sem("out_done")

        dve_passed, sp_passed = sem("dve_passed"), sem("sp_passed")

        JOBS = [("V", 1, 0, v_done, 2, 1), ("V", 1, 1, v_done, 2, 2), ("M", 0, 1, msplit, 16, 6),
                ("XT", 2, 0, xnT_done, 2, 1), ("XT", 2, 1, xnT_done, 2, 2),
                ("WU", -1, 0, res_done, 2, 1), ("WU", -1, 1, res_done, 2, 2),
                ("Q", 2, 0, qk_done, 4, 1), ("M", 0, 2, msplit, 16, 10), ("Q", 2, 1, qk_done, 4, 2),
                ("YT", -1, 0, ynT_done, 2, 1), ("YT", -1, 1, ynT_done, 2, 2),
                ("K", 2, 0, qk_done, 4, 3), ("K", 2, 1, qk_done, 4, 4), ("M", 0, 3, msplit, 16, 14),
                ("FK", -1, 0, relu_done, 2, 1), ("FK", -1, 1, relu_done, 2, 2),
                ("R", -1, 0, tanh_done, 2, 1), ("R", -1, 1, tanh_done, 2, 2), ("M", 1, 0, msplit, 16, 2),
                ("O", -1, 0, gated, 2, 1), ("O", -1, 1, gated, 2, 2)]
        assert len(JOBS) % 2 == 0
        NUMBER = {(name, n): k for k, (name, _, n, *_) in enumerate(JOBS)}
        BANK = {job: k % 2 for job, k in NUMBER.items()}
        DENSE = ["V0", "V1", "XT", "WU0", "WU1", "Q0", "Q1", "YT", "K0", "K1", "FK0", "FK1", "R0", "R1", "O0", "O1"]
        MAX_T = {1: (0, 1), 5: (0, 2), 9: (0, 3), 13: (1, 0)}

        def bank_reader(b, n):
            while True:
                n -= 2
                if n < 0:
                    n += len(JOBS)
                    b = b.plus(-1)
                if b.i is None and b.add < FIRST:
                    return None
                _, d, _, done, per, k = JOBS[n]
                if b.plus(d).active():
                    return done, b.plus(d).count(per, k)

        def steps(eng, body):
            for b in range(FIRST, LOOP_FROM):
                body(Seq(b), b % 2)
            with eng.Fori(0, LOOP_PAIRS) as i:
                for par in range(2):
                    body(Seq(LOOP_FROM + par, i), par)
            for b in range(LOOP_TO, LAST + 1):
                body(Seq(b), b % 2)

        def row_max_at(b, u):
            h = u + LEAD
            return (b, h) if h < H else (b.plus(1), h - H)

        block = ctx.enter_context(nc.Block())

        @block.sync
        def _(sp):
            for w, (name, src) in enumerate((("q", wq), ("k", wk), ("v", wv), ("u", wu), ("r", w_r),
                                             ("fk", w_k), ("fv", w_v))):
                sp.dma_start(probs[:, w // GH, w % GH, :].rearrange("p (o c) -> p o c", o=CB),
                             src.rearrange("(o p) c -> p o c", p=P)).then_inc(w_in, 16)
            sp.dma_start(cos_sb[:, :], cos_t).then_inc(c_in, 16)
            sp.dma_start(sin_sb[:, :], sin_t).then_inc(c_in, 16)
            sp.dma_start(bu_sb[:, :], bu.rearrange("(a c) -> a c", a=1).to_broadcast([P, C])).then_inc(c_in, 16)
            for n, mu in enumerate((mu_r, mu_k)):
                for o in range(CB):
                    sp.dma_start(mu_sb[:, n, o:o + 1],
                                 mu[o * P:(o + 1) * P].rearrange("(p a) -> p a", a=1)).then_inc(c_in, 16)

            def carry_wait(b):
                if b.i is not None:
                    sp.sem_inc(sp_passed, 1)

            def step(b, par):
                def store_out():
                    s = b.plus(-2)
                    if s.active():
                        n = s.index(sp)
                        sp.wait_ge(out_done, s.count(2, 2))
                        carry_wait(b)
                        sp.dma_start(out[n].rearrange("(c p) d -> p c d", p=P),
                                     gate[:, :, :]).then_inc(out_stored, 16)

                def load_stacks():
                    s = b.plus(1)
                    if not s.active():
                        return
                    sp.wait_ge(parts_out, s.count(32, 32))
                    carry_wait(b)
                    if b.plus(-1).has(SCORES, SCORES):
                        sp.wait_ge(st_ready, b.plus(-1).count(SCORES, SCORES))
                    n = 1 - par
                    q_src, k_src = scratch[n, 0], scratch[n, 1]
                    row = 0
                    for part, copies in enumerate((3, 2, 1)):
                        rows = q_src[part * D:(part + 1) * D, :]
                        rep = bass.AP(rows.tensor, rows.offset, [[0, copies]] + [list(a) for a in rows.ap])
                        sp.dma_start(q_st[n][row:row + copies * D, :, :].rearrange("p h t -> p (h t)"),
                                     rep).then_inc(stack_in, 16)
                        sp.dma_start(k_st[n][row:row + copies * D, :, :].rearrange("p h t -> p (h t)"),
                                     k_src[0:copies * D, :]).then_inc(stack_in, 16)
                        row += copies * D

                def move_attn(s, g):
                    if not s.active():
                        return
                    sp.wait_ge(attn_done, s.count(4, g + 1))
                    carry_wait(b)
                    if g == 0:
                        if s.plus(-1).has(2, 2):
                            sp.wait_ge(wu_ready, s.plus(-1).count(2, 2))
                    for j in range(GH):
                        row = (g * GH + j) * D
                        sp.dma_start(attnT[row % P:row % P + D, row // P, :],
                                     attn[32 * j:32 * j + D, :]).then_inc(attn_in, 16)

                def move_max(s, g):
                    if not s.active():
                        return
                    sp.wait_ge(msplit, s.count(16, 4 * g + 4))
                    dst = q_st[(s.add) % 2]
                    for m in range(MROWS):
                        sp.dma_start(dst[SROWS + m:SROWS + m + 1, g * GH:(g + 1) * GH, :]
                                     .rearrange("p h (c t) -> p (h c) t", c=TC),
                                     mparts[:, m, :]).then_inc(mrow_in, 16)

                def load_residual():
                    s = b.plus(-1)
                    if s.active():
                        n = s.index(sp)
                        if b.plus(-2).has(2, 2):
                            sp.wait_ge(out_done, b.plus(-2).count(2, 2))
                        carry_wait(b)
                        sp.dma_start(y[:, :, :], x[n].rearrange("(c p) d -> p c d", p=P)).then_inc(xres_in, 16)

                def load_x():
                    s = b.plus(3)
                    if s.active():
                        n = s.index(sp)
                        sp.wait_ge(xT_ready, b.plus(2).count(2, 2))
                        carry_wait(b)
                        sp.dma_start(xn[:, :, :], x[n].rearrange("(c p) d -> p c d", p=P)).then_inc(x_in, 16)

                def store_parts(t):
                    s = b.plus(2)
                    if s.active():
                        sp.wait_ge(sub2, s.count(2, t + 1))
                        carry_wait(b)
                        if b.has(96, 96):
                            sp.wait_ge(stack_in, b.count(96, 96))
                        sp.dma_start(scratch[par, t].rearrange("(k r i) (h c) -> (i h) (k r) c", k=3, r=2, h=H),
                                     parts[:, t, :, :, :].rearrange("p k r c -> p (k r) c")).then_inc(parts_out, 16)

                load_stacks()
                move_attn(b.plus(-1), 3)
                store_out()
                load_residual()
                move_max(b, 1)
                load_x()
                move_attn(b, 0)
                move_max(b, 2)
                move_attn(b, 1)
                move_max(b, 3)
                store_parts(0)
                move_attn(b, 2)
                move_max(b.plus(1), 0)
                store_parts(1)

            steps(sp, step)
            sp.wait_ge(out_stored, 16 * B)

        @block.gpsimd
        def _(pool):
            nc.gpsimd.memset(ident[:, :], 0.0).then_inc(ident_ok, 1)
            pool.wait_ge(ident_ok, 1)
            nc.gpsimd.affine_select(out=ident[:, :], in_=ident[:, :], compare_op=ALU.not_equal, fill=1.0, base=0,
                                    pattern=[[-1, P]], channel_multiplier=1).then_inc(ident_ok, 1)
            pool.wait_ge(ident_ok, 2)
            for n in range(2):
                nc.gpsimd.memset(v_ext[n][:, :, :], 1.0).then_inc(const_ok, 1)
                pool.wait_ge(const_ok, 2 * n + 1)
                nc.gpsimd.memset(k_st[n][SROWS:SROWS + MROWS, :, :], 1.0).then_inc(const_ok, 1)
                pool.wait_ge(const_ok, 2 * n + 2)
            nc.gpsimd.memset(ynT[:, :, 0:1], 0.0).then_inc(const_ok, 1)
            nc.gpsimd.memset(mhalf[:, :], -0.5).then_inc(const_ok, 1)
            pool.wait_ge(const_ok, 6)
            pool.wait_ge(c_in, 16 * CONSTS)

            def step(b, par):
                def finish():
                    s = b.plus(-2)
                    if s.active():
                        for n in range(2):
                            pool.wait_ge(gated, s.count(2, n + 1))
                            t = gate[:, 2 * n:2 * n + 2, :]
                            nc.gpsimd.tensor_tensor(t, t, y[:, 2 * n:2 * n + 2, :], ALU.add).then_inc(out_done, 1)

                def add_bu():
                    s = b.plus(-1)
                    if s.active():
                        pool.wait_ge(xres_in, s.count(16, 16))
                        for c in range(TC):
                            ins = nc.gpsimd.tensor_tensor(y[:, c, :], y[:, c, :], bu_sb[:, :], ALU.add)
                        ins.then_inc(bu_added, 1)

                def rope_mults(t, r):
                    s = b.plus(2)
                    if s.active():
                        k, keep, other = 6 * t + 2 * r, (sin_sb, cos_sb)[r], (cos_sb, sin_sb)[r]
                        pool.wait_ge(qk_done, s.count(4, 2 * t + r + 1))
                        nc.gpsimd.tensor_tensor(rope_t[:, 2 + r, :], rope_t[:, r, :], keep[:, :],
                                                ALU.mult).then_inc(rope_step, 1)
                        pool.wait_ge(rope_step, s.count(12, k + 1))
                        nc.gpsimd.tensor_tensor(rope_t[:, r, :], rope_t[:, r, :], other[:, :],
                                                ALU.mult).then_inc(rope_step, 1)

                def rope_sums(t):
                    s = b.plus(2)
                    if s.active():
                        if s.has(2, t):
                            pool.wait_ge(sub2, s.count(2, t))
                        pool.wait_ge(rope_step, s.count(12, 6 * t + 4))
                        nc.gpsimd.tensor_tensor(rot[:, 0, :], rope_t[:, 0, :], rope_t[:, 1, :],
                                                ALU.subtract).then_inc(rope_step, 1)
                        nc.gpsimd.tensor_tensor(rot[:, 1, :], rope_t[:, 2, :], rope_t[:, 3, :],
                                                ALU.add).then_inc(rope_step, 1)

                def rest1(t):
                    s = b.plus(2)
                    if s.active():
                        pool.wait_ge(hi_done, s.count(2, t + 1))
                        nc.gpsimd.tensor_tensor(rot[:, :, :], rot[:, :, :], parts[:, t, 0, :, :],
                                                ALU.subtract).then_inc(sub1, 1)

                def rest2(t):
                    s = b.plus(2)
                    if s.active():
                        pool.wait_ge(lo_done, s.count(2, t + 1))
                        nc.gpsimd.tensor_tensor(parts[:, t, 2, :, :], rot[:, :, :], parts[:, t, 1, :, :],
                                                ALU.subtract).then_inc(sub2, 1)

                def difference():
                    s = b.plus(-1)
                    if s.active():
                        pool.wait_ge(ynT_done, s.count(2, 2))
                        if s.plus(-1).has(2, 2):
                            pool.wait_ge(r_ready, s.plus(-1).count(2, 2))
                        nc.gpsimd.tensor_tensor(xrT[:, :, :], ynT[:, :, 1:T + 1], ynT[:, :, 0:T],
                                                ALU.subtract).then_inc(diff_done, 1)

                def scales(s, n, stat, scale, ve, mean, rs, nm):
                    if s.active():
                        a, z = 2 * n, 2 * n + 2
                        pool.wait_ge(stat, s.count(6, 3 * n + 3))
                        nc.gpsimd.tensor_tensor(rs[:, a:z], ve[:, a:z], mhalf[:, :], ALU.pow).then_inc(scale, 1)
                        pool.wait_ge(scale, s.count(4, 2 * n + 1))
                        nc.gpsimd.tensor_tensor(nm[:, a:z], mean[:, a:z], rs[:, a:z], ALU.mult).then_inc(scale, 1)

                def square(o):
                    s = b.plus(-1)
                    if s.active():
                        pool.wait_ge(relu_done, s.count(2, o + 1))
                        nc.gpsimd.tensor_tensor(kT[:, o, :], kT[:, o, :], kT[:, o, :], ALU.mult).then_inc(ksq_done, 1)

                finish()
                add_bu()
                for n in range(2):
                    scales(b.plus(-1), n, ln2_stat, ln2_scale, ve2, mean2, rs2, nm2)
                rope_mults(0, 0)
                rope_mults(0, 1)
                rope_sums(0)
                difference()
                rest1(0)
                for n in range(2):
                    scales(b.plus(3), n, ln1_stat, ln1_scale, ve1, mean1, rs1, nm1)
                rope_mults(1, 0)
                rest2(0)
                rope_mults(1, 1)
                rope_sums(1)
                square(0)
                square(1)
                rest1(1)
                rest2(1)

            steps(pool, step)

        @block.scalar
        def _(act):
            def step(b, par):
                def v_evac(n):
                    s = b.plus(1)
                    if s.active():
                        act.wait_ge(v_ready, s.count(2, n + 1))
                        if b.plus(-1).has(UNITS, UNITS):
                            act.wait_ge(pv_done, b.plus(-1).count(UNITS, UNITS))
                        nc.scalar.activation(
                            v_ext[1 - par][:, 2 * n:2 * n + 2, 0:H * VW].rearrange("p c (h d) -> p c h d", h=H)[:, :, :, 0:D],
                            d_ps[:, BANK["V", n], :].rearrange("p (c h d) -> p c h d", c=2, h=H), ACT.Copy).then_inc(v_done, 1)

                def xT_evac(n):
                    s = b.plus(2)
                    if s.active():
                        act.wait_ge(xT_ready, s.count(2, n + 1))
                        if s.plus(-1).has(2, 2):
                            act.wait_ge(v_ready, s.plus(-1).count(2, 2))
                        nc.scalar.activation(xnT[:, n, :], d_ps[:, BANK["XT", n], :], ACT.Copy).then_inc(xnT_done, 1)

                def yT_evac(n):
                    s = b.plus(-1)
                    if s.active():
                        act.wait_ge(yT_ready, s.count(2, n + 1))
                        if s.plus(-1).has(4, 4):
                            act.wait_ge(shift_done, s.plus(-1).count(4, 4))
                        nc.scalar.activation(ynT[:, n, 1:T + 1], d_ps[:, BANK["YT", n], :], ACT.Copy).then_inc(ynT_done, 1)

                def norm1(n):
                    s = b.plus(3)
                    if s.active():
                        act.wait_ge(ln1_scale, s.count(4, 2 * n + 2))
                        for c in (2 * n, 2 * n + 1):
                            nc.scalar.activation(xn[:, c, :], xn[:, c, :], ACT.Identity, scale=rs1[:, c:c + 1],
                                                 bias=nm1[:, c:c + 1]).then_inc(xn_done, 1)

                def norm2(n):
                    s = b.plus(-1)
                    if s.active():
                        act.wait_ge(ln2_scale, s.count(4, 2 * n + 2))
                        if s.plus(-1).has(2, 2):
                            act.wait_ge(yT_ready, s.plus(-1).count(2, 2))
                        for c in (2 * n, 2 * n + 1):
                            nc.scalar.activation(yn[:, c, :], y[:, c, :], ACT.Identity, scale=rs2[:, c:c + 1],
                                                 bias=nm2[:, c:c + 1]).then_inc(yn_done, 1)

                def qk_evac(t, r):
                    s = b.plus(2)
                    if s.active():
                        act.wait_ge(qk_ready, s.count(4, 2 * t + r + 1))
                        if s.has(12, 6 * t):
                            act.wait_ge(rope_step, s.count(12, 6 * t))
                        nc.scalar.activation(rope_t[:, r, :], d_ps[:, BANK["QK"[t], r], :],
                                             ACT.Copy).then_inc(qk_done, 1)

                def high(t):
                    s = b.plus(2)
                    if s.active():
                        act.wait_ge(rope_step, s.count(12, 6 * t + 6))
                        if s.plus(-1).has(32, 32):
                            act.wait_ge(parts_out, s.plus(-1).count(32, 32))
                        nc.scalar.activation(parts[:, t, 0, :, :], rot[:, :, :], ACT.Copy).then_inc(hi_done, 1)

                def middle(t):
                    s = b.plus(2)
                    if s.active():
                        act.wait_ge(sub1, s.count(2, t + 1))
                        nc.scalar.activation(parts[:, t, 1, :, :], rot[:, :, :], ACT.Copy).then_inc(lo_done, 1)

                def relu(n):
                    s = b.plus(-1)
                    if s.active():
                        act.wait_ge(k_ready, s.count(2, n + 1))
                        if s.plus(-1).has(2, 2):
                            act.wait_ge(o_ready, s.plus(-1).count(2, 2))
                        nc.scalar.activation(kT[:, n, :], d_ps[:, BANK["FK", n], :], ACT.Relu).then_inc(relu_done, 1)

                def tanh(n):
                    s = b.plus(-1)
                    if s.active():
                        act.wait_ge(r_ready, s.count(2, n + 1))
                        if s.has(16, 0):
                            act.wait_ge(out_stored, s.count(16, 0))
                        nc.scalar.activation(gate[:, 2 * n:2 * n + 2, :].rearrange("p c d -> p (c d)"),
                                             d_ps[:, BANK["R", n], :], ACT.Tanh, scale=0.5).then_inc(tanh_done, 1)

                extras = {(0, 3): [(v_evac, 0)], (1, 3): [(v_evac, 1)], (2, 3): [(xT_evac, 0), (xT_evac, 1)],
                          (5, 1): [(norm2, 0)], (5, 3): [(qk_evac, 0, 0)], (6, 1): [(norm2, 1)],
                          (6, 3): [(qk_evac, 0, 1)], (7, 3): [(yT_evac, 0), (yT_evac, 1)],
                          (8, 2): [(high, 0)], (8, 3): [(qk_evac, 1, 0)], (9, 3): [(qk_evac, 1, 1)],
                          (10, 1): [(middle, 0)], (10, 3): [(relu, 0)], (11, 3): [(relu, 1)],
                          (12, 3): [(tanh, 0)], (13, 1): [(high, 1)], (13, 3): [(tanh, 1)],
                          (14, 1): [(norm1, 0)], (14, 3): [(middle, 1)], (15, 1): [(norm1, 1)]}
                for u in range(UNITS):
                    for j in range(GH):
                        if b.active():
                            n = GH * u + j
                            act.wait_ge(st_ready, b.count(SCORES, n + 1))
                            if j == 0:
                                if b.has(UNITS, u - SLOTS + 1):
                                    act.wait_ge(pv_done, b.count(UNITS, u - SLOTS + 1))
                            nc.scalar.activation(probs[:, u % SLOTS, j, :], st_ps[:, n % 2, :], ACT.Exp,
                                                 scale=float(D) ** -0.5).then_inc(exp_done, 1)
                        for f, *args in extras.get((u, j), []):
                            f(*args)

            steps(act, step)

        @block.vector
        def _(dve):
            for w, name in enumerate(("q", "k", "v", "u", "r", "fk", "fv")):
                dve.wait_ge(wT_ready, w + 1)
                src = d_ps[:, w % 2, :].rearrange("p (o i c) -> p o i c", o=CB, i=CB)
                for o in range(CB):
                    for i in range(CB):
                        if name in ("q", "k"):
                            dst = wT[name][:, i, :].rearrange("p (r i h) -> p r i h", r=2, h=H)[:, :, :, o * 8:o * 8 + 8]
                            ins = nc.vector.tensor_copy(dst, src[:, o, i, :].rearrange("p (h i r) -> p r i h", i=HALF, r=2))
                        elif name == "fv":
                            ins = nc.vector.tensor_scalar(wT[name][:, i, o * P:(o + 1) * P], src[:, o, i, :], 0.5,
                                                          None, ALU.mult)
                        else:
                            ins = nc.vector.tensor_copy(wT[name][:, i, o * P:(o + 1) * P], src[:, o, i, :])
                ins.then_inc(wT_done, 1)
            dve.wait_ge(c_in, 16 * CONSTS)

            def step(b, par):
                def row_max(u, qc):
                    s, h = row_max_at(b, u)
                    if s.active():
                        n = h * TC + qc
                        dve.wait_ge(s_ready, s.count(SCORES, n + 1))
                        nc.vector.tensor_reduce(mx[:, n:n + 1], s_ps[:, n % 2, :], AX.X, ALU.max).then_inc(max_done, 1)

                def split_max(s, g, half):
                    if not s.active():
                        return
                    m = d_ps[0:GH * TC, BANK["M", g], 0:P]
                    if half == 0:
                        dve.wait_ge(mt_ready, s.count(4, g + 1))
                        if s.has(48 * NG, 48 * g):
                            dve.wait_ge(mrow_in, s.count(48 * NG, 48 * g))
                        nc.vector.tensor_scalar(mparts[:, 0, :], m, -1.0, None, ALU.mult).then_inc(msplit, 1)
                        dve.wait_ge(msplit, s.count(16, 4 * g + 1))
                        nc.vector.scalar_tensor_tensor(out=mres[:, :], in0=m, scalar=-1.0, in1=mparts[:, 0, :],
                                                       op0=ALU.mult, op1=ALU.subtract).then_inc(msplit, 1)
                    else:
                        dve.wait_ge(msplit, s.count(16, 4 * g + 2))
                        nc.vector.tensor_copy(mparts[:, 1, :], mres[:, :]).then_inc(msplit, 1)
                        dve.wait_ge(msplit, s.count(16, 4 * g + 3))
                        nc.vector.tensor_tensor(mparts[:, 2, :], mres[:, :], mparts[:, 1, :],
                                                ALU.subtract).then_inc(msplit, 1)

                def normalise(s, g, stage):
                    if not s.active():
                        return
                    blocks = sums[:, :].rearrange("p (k r) -> p k r", r=32)
                    if stage == 0:
                        dve.wait_ge(pv_done, s.count(UNITS, TC * (g + 1)))
                        if s.has(NG, g):
                            dve.wait_ge(attn_done, s.count(NG, g))
                        nc.vector.transpose(sums[:, :], pv_ps[:, g % 2, :]).then_inc(norm_step, 1)
                    elif stage == 1:
                        dve.wait_ge(norm_step, s.count(3 * NG, 3 * g + 1))
                        nc.vector.reciprocal(inv[:, :], blocks[:, :, D]).then_inc(norm_step, 1)
                        dve.wait_ge(norm_step, s.count(3 * NG, 3 * g + 2))
                        nc.vector.tensor_tensor(blocks[:, :, 0:D], blocks[:, :, 0:D],
                                                inv[:, :].rearrange("p (k r) -> p k r", r=1)
                                                .to_broadcast([P, T // 32, D]), ALU.mult).then_inc(norm_step, 1)
                    else:
                        dve.wait_ge(norm_step, s.count(3 * NG, 3 * g + 3))
                        if s.has(64 * NG, 64 * g):
                            dve.wait_ge(attn_in, s.count(64 * NG, 64 * g))
                        nc.vector.transpose(attn[:, :], sums[:, :]).then_inc(attn_done, 1)

                def residual(n):
                    s = b.plus(-1)
                    if not s.active():
                        return
                    if n == 0:
                        dve.wait_ge(bu_added, s.count(1, 1))
                    dve.wait_ge(wu_ready, s.count(2, n + 1))
                    t = y[:, 2 * n:2 * n + 2, :].rearrange("p c d -> p (c d)")
                    nc.vector.tensor_tensor(t, d_ps[:, BANK["WU", n], :], t, ALU.add).then_inc(res_done, 1)

                def layer_stats(s, n, stage, done, src, stats, mv, ve, nm, used):
                    a, z = 2 * n, 2 * n + 2
                    chunks, per, k = range(a, z), 6, 3 * n
                    if stage == 0:
                        for c in chunks:
                            ins = nc.vector.bn_stats(stats[:, c, :], src[:, c, :])
                        ins.then_inc(done, 1)
                        return
                    dve.wait_ge(done, s.count(per, k + 1))
                    dve.sem_inc(dve_passed, 1)
                    for c in chunks:
                        ins = nc.vector.bn_aggr(mv[:, c, :], stats[:, c, :])
                    ins.then_inc(done, 1)
                    dve.wait_ge(done, s.count(per, k + 2))
                    if s.plus(-1).has(4, 4):
                        dve.wait_ge(used, s.plus(-1).count(4, 4))
                    nc.vector.tensor_scalar(ve[:, a:z], mv[:, a:z, 1], EPS, None, ALU.add)
                    nc.vector.tensor_scalar(nm[:, a:z], mv[:, a:z, 0], -1.0, None, ALU.mult).then_inc(done, 1)

                def stats1_of(n, stage):
                    s = b.plus(3)
                    if s.active():
                        if stage == 0:
                            dve.wait_ge(x_in, s.count(16, 16))
                        layer_stats(s, n, stage, ln1_stat, xn, stats1, mv1, ve1, mean1, xn_done)

                def stats2_of(n, stage):
                    s = b.plus(-1)
                    if s.active():
                        if stage == 0:
                            dve.wait_ge(res_done, s.count(2, n + 1))
                        layer_stats(s, n, stage, ln2_stat, y, stats2, mv2, ve2, mean2, yn_done)

                def shift(n, o):
                    s = b.plus(-1)
                    if not s.active():
                        return
                    if n == 1 and o == 0:
                        dve.wait_ge(diff_done, s.count(1, 1))
                        if s.plus(-1).has(2, 2):
                            dve.wait_ge(k_ready, s.plus(-1).count(2, 2))
                    dst = (xrT, xkT)[n]
                    nc.vector.scalar_tensor_tensor(out=dst[:, o, :], in0=xrT[:, o, :], in1=ynT[:, o, 0:T],
                                                   scalar=mu_sb[:, n, o:o + 1], op0=ALU.mult,
                                                   op1=ALU.add).then_inc(shift_done, 1)

                def gate_v(s, n):
                    if s.active():
                        dve.wait_ge(o_ready, s.count(2, n + 1))
                        dve.wait_ge(tanh_done, s.count(2, n + 1))
                        t = gate[:, 2 * n:2 * n + 2, :].rearrange("p c d -> p (c d)")
                        nc.vector.scalar_tensor_tensor(out=t, in0=t, scalar=1.0, in1=d_ps[:, BANK["O", n], :],
                                                       op0=ALU.add, op1=ALU.mult).then_inc(gated, 1)

                prev, nxt = b.plus(-1), b.plus(1)
                extras = {(1, 0): [(normalise, prev, 3, 0)], (1, 1): [(normalise, prev, 3, 1)],
                          (1, 2): [(normalise, prev, 3, 2)],
                          (2, 0): [(split_max, b, 1, 0)], (2, 1): [(split_max, b, 1, 1)],
                          (3, 3): [(residual, 0)], (4, 0): [(stats2_of, 0, 0)], (4, 1): [(stats2_of, 0, 1)],
                          (4, 3): [(residual, 1)], (5, 0): [(stats2_of, 1, 0)], (5, 1): [(stats2_of, 1, 1)],
                          (5, 2): [(normalise, b, 0, 0)], (5, 3): [(normalise, b, 0, 1)],
                          (6, 0): [(normalise, b, 0, 2)],
                          (6, 1): [(split_max, b, 2, 0)], (6, 2): [(split_max, b, 2, 1)],
                          (7, 0): [(stats1_of, 0, 0)], (7, 1): [(stats1_of, 0, 1)],
                          (7, 2): [(stats1_of, 1, 0)], (7, 3): [(stats1_of, 1, 1)],
                          (8, 3): [(shift, 1, 0)], (9, 0): [(shift, 1, 1)],
                          (9, 1): [(normalise, b, 1, 0)], (9, 2): [(normalise, b, 1, 1)],
                          (9, 3): [(normalise, b, 1, 2)],
                          (10, 0): [(split_max, b, 3, 0)], (10, 1): [(split_max, b, 3, 1)],
                          (10, 2): [(shift, 0, 0)], (10, 3): [(shift, 0, 1)],
                          (13, 0): [(normalise, b, 2, 0)], (13, 1): [(normalise, b, 2, 1)],
                          (13, 2): [(normalise, b, 2, 2)],
                          (14, 0): [(split_max, nxt, 0, 0)], (14, 1): [(split_max, nxt, 0, 1)],
                          (14, 3): [(gate_v, prev, 0)], (15, 3): [(gate_v, prev, 1)]}
                for u in range(UNITS):
                    for qc in range(TC):
                        row_max(u, qc)
                        for f, *args in extras.get((u, qc), []):
                            f(*args)

            steps(dve, step)

        @block.tensor
        def _(pe):
            pe.wait_ge(ident_ok, 2)
            pe.wait_ge(w_in, 16 * 7)
            for w in range(7):
                if w >= 2:
                    pe.wait_ge(wT_done, w - 1)
                src = probs[:, w // GH, w % GH, :].rearrange("p (o c) -> p o c", o=CB)
                for o in range(CB):
                    for i in range(CB):
                        ins = nc.tensor.transpose(d_ps[:, w % 2, (o * CB + i) * P:(o * CB + i + 1) * P],
                                                  src[:, o, i * P:(i + 1) * P], ident[:, :])
                ins.then_inc(wT_ready, 1)
            pe.wait_ge(wT_done, 7)
            pe.wait_ge(const_ok, 6)

            def step(b, par):
                def score_T(u, j):
                    if not b.active():
                        return
                    g, c = divmod(u, TC)
                    n, h = GH * u + j, GH * g + j
                    if c == 0 and j == 0:
                        pe.wait_ge(mrow_in, b.count(48 * NG, 48 * (g + 1)))
                    if b.has(SCORES, n - 1):
                        pe.wait_ge(exp_done, b.count(SCORES, n - 1))
                    nc.tensor.matmul(st_ps[:, n % 2, :], k_st[par][0:SROWS + MROWS, h, c * P:(c + 1) * P],
                                     q_st[par][0:SROWS + MROWS, h, :], start=True, stop=True).then_inc(st_ready, 1)

                def score(u, qc):
                    s, h = row_max_at(b, u)
                    if not s.active():
                        return
                    n, half = h * TC + qc, s.add % 2
                    if n == 0:
                        pe.wait_ge(stack_in, s.count(96, 96))
                    if s.has(SCORES, n - 1):
                        pe.wait_ge(max_done, s.count(SCORES, n - 1))
                    nc.tensor.matmul(s_ps[:, n % 2, :], q_st[half][0:SROWS, h, qc * P:(qc + 1) * P],
                                     k_st[half][0:SROWS, h, :], start=True, stop=True).then_inc(s_ready, 1)

                def values(s, half, u):
                    if not s.active():
                        return
                    g, c = divmod(u, TC)
                    pe.wait_ge(exp_done, s.count(SCORES, GH * (u + 1)))
                    if u == 0:
                        pe.wait_ge(v_done, s.count(2, 2))
                    if c == 0 and s.has(3 * NG, 3 * g - 5):
                        pe.wait_ge(norm_step, s.count(3 * NG, 3 * g - 5))
                    for j in range(GH):
                        h = GH * g + j
                        ins = nc.tensor.matmul(pv_ps[32 * j:32 * j + 32, g % 2, :], v_ext[half][:, c, VW * h:VW * h + 32],
                                               probs[:, u % SLOTS, j, :], start=(c == 0), stop=(c == TC - 1))
                    ins.then_inc(pv_done, 1)

                def open_bank(name, n):
                    free = bank_reader(b, NUMBER[name, n])
                    if free is not None:
                        pe.wait_ge(free[0], free[1])
                    return d_ps[:, BANK[name, n], :]

                def row_max_T(s, g):
                    if not s.active():
                        return
                    pe.wait_ge(max_done, s.count(SCORES, GH * TC * (g + 1)))
                    w = GH * TC
                    bank = open_bank("M", g)
                    nc.tensor.transpose(bank[0:w, 0:P], mx[:, g * w:(g + 1) * w], ident[:, :]).then_inc(mt_ready, 1)

                def turn(s, name, n, src, src_done, done):
                    if not s.active():
                        return
                    bank = open_bank(name, n)
                    pe.wait_ge(src_done, s.count(4, 4))
                    for c in range(TC):
                        ins = nc.tensor.transpose(bank[:, c * P:(c + 1) * P], src[:, c, n * P:(n + 1) * P], ident[:, :])
                    ins.then_inc(done, 1)

                def channel_rows(s, name, n, i, w, src, src_done, per, k, done):
                    if not s.active():
                        return
                    bank = open_bank(name, n) if i == 0 else d_ps[:, BANK[name, n], :]
                    if i == 0:
                        pe.wait_ge(src_done, s.count(per, k))
                    ins = nc.tensor.matmul(bank, w[:, i, n * P:(n + 1) * P], src[:, i, :],
                                           start=(i == 0), stop=(i == CB - 1))
                    if i == CB - 1:
                        ins.then_inc(done, 1)

                def token_rows(s, name, n, m, w, src, src_done, per, k, done):
                    if not s.active():
                        return
                    bank = open_bank(name, n) if m == 0 else d_ps[:, BANK[name, n], :]
                    if m == 0:
                        pe.wait_ge(src_done, s.count(per, k))
                    c = 2 * n + m
                    for i in range(CB):
                        ins = nc.tensor.matmul(bank[:, m * C:(m + 1) * C], src[:, i, c * P:(c + 1) * P],
                                               w[:, i, :], start=(i == 0), stop=(i == CB - 1))
                    if m == 1:
                        ins.then_inc(done, 1)

                def dense(u, half):
                    name = DENSE[u]
                    prev = b.plus(-1)
                    if name == "XT":
                        turn(b.plus(2), "XT", half, xn, xn_done, xT_ready)
                    elif name == "YT":
                        turn(prev, "YT", half, yn, yn_done, yT_ready)
                    elif name[:-1] in ("Q", "K"):
                        channel_rows(b.plus(2), name[0], int(name[1]), half, wT[name[0].lower()], xnT, xnT_done, 2, 2, qk_ready)
                    elif name[:-1] == "FK":
                        channel_rows(prev, "FK", int(name[-1]), half, wT["fk"], xkT, shift_done, 4, 2, k_ready)
                    elif name[:-1] == "V":
                        token_rows(b.plus(1), "V", int(name[-1]), half, wT["v"], xnT, xnT_done, 2, 2, v_ready)
                    elif name[:-1] == "WU":
                        token_rows(prev, "WU", int(name[-1]), half, wT["u"], attnT, attn_in, 64 * NG, 64 * NG, wu_ready)
                    elif name[:-1] == "R":
                        token_rows(prev, "R", int(name[-1]), half, wT["r"], xrT, shift_done, 4, 4, r_ready)
                    elif name[:-1] == "O":
                        token_rows(prev, "O", int(name[-1]), half, wT["fv"], kT, ksq_done, 2, 2, o_ready)

                for u in range(UNITS):
                    for j in range(GH):
                        score_T(u, j)
                        score(u, j)
                        if j in (1, 2):
                            dense(u, j - 1)
                    if u == 0:
                        values(b.plus(-1), 1 - par, UNITS - 1)
                    else:
                        values(b, par, u - 1)
                    if u in MAX_T:
                        d, g = MAX_T[u]
                        row_max_T(b.plus(d), g)

            steps(pe, step)


_INS = ["L0_attn_x", "L0_attn_Wq", "L0_attn_Wk", "L0_attn_Wv", "L0_attn_Wu", "L0_attn_bu",
        "L0_ffn_W_r", "L0_ffn_W_k", "L0_ffn_W_v", "L0_ffn_mu_r", "L0_ffn_mu_k"]


def kernel(**inputs):
    import numpy as np
    import concourse.bacc as bacc
    from concourse.bass_utils import run_bass_kernel_spmd

    half = C // 2
    theta = (np.float32(1.0) / np.float32(10000.0) ** (np.arange(half, dtype=np.float32) / np.float32(half))).astype(np.float32)
    angle = np.arange(T, dtype=np.float32)[None, :] * theta[:, None]
    order = np.arange(half).reshape(H, HALF).T.reshape(-1)
    tables = {"cos": np.cos(angle)[order].astype(np.float32), "sin": np.sin(angle)[order].astype(np.float32)}

    nc = bacc.Bacc("TRN2", target_bir_lowering=False, num_devices=1)
    arrays, args = {}, []
    for name, a in [(n, inputs[n]) for n in _INS] + list(tables.items()):
        a = np.ascontiguousarray(a)
        arrays[f"in_{name}_dram"] = a
        args.append(nc.dram_tensor(f"in_{name}_dram", a.shape, mybir.dt.from_np(a.dtype), kind="ExternalInput").ap())
    args.append(nc.dram_tensor("out_0_dram", (B, T, C), F32, kind="ExternalOutput").ap())
    layer_kernel(nc, *args)
    r = run_bass_kernel_spmd(nc, [arrays], core_ids=[0])
    return r.results[0]["out_0_dram"]
```

```python
from contextlib import ExitStack

import concourse.bass as bass
from concourse import mybir

ALU = mybir.AluOpType
ACT = mybir.ActivationFunctionType
AX = mybir.AxisListType
F32 = mybir.dt.float32
F32R = mybir.dt.float32r
BF16 = mybir.dt.bfloat16

P = 128
B, T, C = 32, 512, 256
H, D = 16, 16
HALF = D // 2
CB = C // P
TC = T // P
GH = 4
NG = H // GH
UNITS = NG * TC
SCORES = UNITS * GH
LEAD = 7
COPIES = 6
SROWS = COPIES * D
MROWS = 3
VW = D + 1
SLOTS = 2
EPS = 1e-5
FIRST, LAST = -3, B + 1
LOOP_FROM, LOOP_PAIRS = 2, 13
CONSTS = 7
LOOP_TO = LOOP_FROM + 2 * LOOP_PAIRS


class Seq:

    def __init__(self, add, i=None):
        self.add, self.i = add, i

    def plus(self, d):
        return Seq(self.add + d, self.i)

    def active(self):
        return self.i is not None or 0 <= self.add < B

    def index(self, eng):
        return self.add if self.i is None else eng.snap(self.i * 2 + self.add)

    def has(self, per, n):
        return self.i is not None or per * self.add + n > 0

    def count(self, per, n):
        if self.i is None:
            return min(max(per * self.add + n, 0), per * B)
        assert per * self.add + n > 0
        return self.i * (2 * per) + (per * self.add + n)


def layer_kernel(nc, x, wq, wk, wv, wu, bu, w_r, w_k, w_v, mu_r, mu_k, cos_t, sin_t, out):
    scratch = nc.dram_tensor("parts_scratch", [2, 2, 3 * D, H * T], BF16)
    with ExitStack() as ctx:
        def sb(name, shape, dt=F32):
            return ctx.enter_context(nc.sbuf_tensor(name, shape, dt))

        def sem(name):
            return ctx.enter_context(nc.semaphore(name))

        ident = sb("ident", [P, P])
        WEIGHTS = ("q", "k", "v", "u", "r", "fk", "fv")
        w_hi = {n: sb("w_hi_" + n, [P, CB, C], F32R) for n in WEIGHTS}
        w_lo = {n: sb("w_lo_" + n, [P, CB, C], F32R) for n in WEIGHTS}
        cos_sb = sb("cos_sb", [P, T])
        sin_sb = sb("sin_sb", [P, T])
        bu_sb = sb("bu_sb", [P, C])
        mhalf = sb("mhalf", [P, 2])
        mu_sb = sb("mu_sb", [P, 2, CB])
        q_st = [sb(f"q_st{n}", [P, H, T], BF16) for n in range(2)]
        k_st = [sb(f"k_st{n}", [P, H, T], BF16) for n in range(2)]
        v_ext = [sb(f"v_ext{n}", [P, TC, H * VW + 32 - VW]) for n in range(2)]
        probs = sb("probs", [P, SLOTS, GH, T])
        xn = sb("xn", [P, TC, C])
        xnT_hi = sb("xnT_hi", [P, CB, T], F32R)
        xnT_lo = sb("xnT_lo", [P, CB, T], F32R)
        stats1 = sb("stats1", [P, TC, 6])
        mv1 = sb("mv1", [P, TC, 2])
        rs1 = sb("rs1", [P, TC])
        nm1 = sb("nm1", [P, TC])
        ve1 = sb("ve1", [P, TC])
        mean1 = sb("mean1", [P, TC])
        rope_t = sb("rope_t", [P, 2, T])
        rot = sb("rot", [P, 2, 2, T])
        parts = sb("parts", [P, 2, 3, 2, T], BF16)
        mx = sb("mx", [P, H * TC])
        mres = sb("mres", [GH * TC, P])
        mparts = sb("mparts", [GH * TC, MROWS, P], BF16)
        inv = sb("inv", [P, T // 32])
        attn = sb("attn", [P, T])
        attnT = sb("attnT", [P, CB, T])
        y = [sb(f"y{n}", [P, TC, C]) for n in range(2)]
        yn = sb("yn", [P, TC, C])
        ynT = sb("ynT", [P, CB, T + 1])
        sums = ynT[:, 0, 1:T + 1]
        stats2 = sb("stats2", [P, TC, 6])
        mv2 = sb("mv2", [P, TC, 2])
        rs2 = sb("rs2", [P, TC])
        nm2 = sb("nm2", [P, TC])
        ve2 = sb("ve2", [P, TC])
        mean2 = sb("mean2", [P, TC])
        mixT = yn[:, :, :].rearrange("p (o c) d -> p o (c d)", o=CB)
        xrT = sb("xrT", [P, CB, T])
        r_hi = sb("r_hi", [P, CB, T], F32R)
        r_lo = sb("r_lo", [P, CB, T], F32R)
        f_hi = sb("f_hi", [P, CB, T], F32R)
        f_lo = sb("f_lo", [P, CB, T], F32R)
        gate = sb("gate", [P, TC, C])

        st_ps = ctx.enter_context(nc.psum_tensor("st_ps", [P, 2, T], F32))
        s_ps = ctx.enter_context(nc.psum_tensor("s_ps", [P, 2, T], F32))
        pv_ps = ctx.enter_context(nc.psum_tensor("pv_ps", [P, 2, T], F32))
        d_ps = ctx.enter_context(nc.psum_tensor("d_ps", [P, 2, T], F32))

        w_qk_in, w_in, c_in, ident_ok, const_ok = sem("w_qk_in"), sem("w_in"), sem("c_in"), sem("ident_ok"), sem("const_ok")
        wT_ready, w_hi_done, wT_done = sem("wT_ready"), sem("w_hi_done"), sem("wT_done")
        x_in, xres_in, parts_out, stack_in = sem("x_in"), sem("xres_in"), sem("parts_out"), sem("stack_in")
        mrow_in, attn_in, out_stored = sem("mrow_in"), sem("attn_in"), sem("out_stored")
        st_ready, s_ready, pv_done = sem("st_ready"), sem("s_ready"), sem("pv_done")
        xT_ready, qk_ready, v_ready = sem("xT_ready"), sem("qk_ready"), sem("v_ready")
        mt_ready, wu_ready, yT_ready = sem("mt_ready"), sem("wu_ready"), sem("yT_ready")
        k_ready, r_ready, o_ready = sem("k_ready"), sem("r_ready"), sem("o_ready")
        exp_done, xn_done, xnT_done = sem("exp_done"), sem("xn_done"), sem("xnT_done")
        v_done, hi_done, lo_done = sem("v_done"), sem("hi_done"), sem("lo_done")
        yn_done, ynT_done = sem("yn_done"), sem("ynT_done")
        xnT_split = sem("xnT_split")
        r_hi_done, r_lo_done = sem("r_hi_done"), sem("r_lo_done")
        f_hi_done, f_lo_done = sem("f_hi_done"), sem("f_lo_done")
        a_hi_done, a_lo_done = sem("a_hi_done"), sem("a_lo_done")
        relu_done, tanh_done = sem("relu_done"), sem("tanh_done")
        max_done, msplit = sem("max_done"), sem("msplit")
        ln1_stat, ln2_stat = sem("ln1_stat"), sem("ln2_stat")
        ln1_scale, ln2_scale = sem("ln1_scale"), sem("ln2_scale")
        norm_step, attn_done = sem("norm_step"), sem("attn_done")
        res_done, gated = sem("res_done"), sem("gated")
        qk_done, rope_step = sem("qk_done"), sem("rope_step")
        sub1, sub2 = sem("sub1"), sem("sub2")
        bu_added, diff_done, shift_done = sem("bu_added"), sem("diff_done"), sem("shift_done")
        ksq_done, out_done = sem("ksq_done"), sem("out_done")

        dve_passed, sp_passed = sem("dve_passed"), sem("sp_passed")

        JOBS = [("O", -2, 1, gated, 2, 2), ("V", 1, 0, v_done, 2, 1), ("M", 0, 1, msplit, 16, 6),
                ("V", 1, 1, v_done, 2, 2), ("XT", 2, 0, xnT_split, 2, 1), ("XT", 2, 1, xnT_split, 2, 2),
                ("WU", -1, 0, res_done, 2, 1), ("WU", -1, 1, res_done, 2, 2), ("M", 0, 2, msplit, 16, 10),
                ("Q", 2, 0, qk_done, 4, 1), ("Q", 2, 1, qk_done, 4, 2),
                ("YT", -1, 0, ynT_done, 2, 1), ("YT", -1, 1, ynT_done, 2, 2),
                ("K", 2, 0, qk_done, 4, 3), ("M", 0, 3, msplit, 16, 14), ("K", 2, 1, qk_done, 4, 4),
                ("FK", -1, 0, relu_done, 2, 1), ("FK", -1, 1, relu_done, 2, 2),
                ("R", -1, 0, tanh_done, 2, 1), ("M", 1, 0, msplit, 16, 2), ("R", -1, 1, tanh_done, 2, 2),
                ("O", -1, 0, gated, 2, 1)]
        assert len(JOBS) % 2 == 0
        NUMBER = {(name, n): k for k, (name, _, n, *_) in enumerate(JOBS)}
        BANK = {job: k % 2 for job, k in NUMBER.items()}
        DENSE = ["O1", "V0", "V1", "XT", "WU0", "WU1", "Q0", "Q1", "YT", "K0", "K1", "FK0", "FK1", "R0", "R1", "O0"]
        MAX_T = {1: (0, 1), 5: (0, 2), 9: (0, 3), 13: (1, 0)}

        def bank_reader(b, n):
            while True:
                n -= 2
                if n < 0:
                    n += len(JOBS)
                    b = b.plus(-1)
                if b.i is None and b.add < FIRST:
                    return None
                _, d, _, done, per, k = JOBS[n]
                if b.plus(d).active():
                    return done, b.plus(d).count(per, k)

        def weight_bank(w):
            return (d_ps, st_ps, s_ps, pv_ps)[w // 2][:, w % 2, :]

        def steps(eng, body, first=FIRST):
            for b in range(first, LOOP_FROM):
                body(Seq(b), b % 2)
            with eng.Fori(0, LOOP_PAIRS) as i:
                for par in range(2):
                    body(Seq(LOOP_FROM + par, i), par)
            for b in range(LOOP_TO, LAST + 1):
                body(Seq(b), b % 2)

        def first(s):
            return s.i is None and s.add == 0

        def row_max_at(b, u):
            h = u + LEAD
            return (b, h) if h < H else (b.plus(1), h - H)

        block = ctx.enter_context(nc.Block())

        @block.sync
        def _(sp):
            sp.dma_start(xn[:, :, :], x[0].rearrange("(c p) d -> p c d", p=P)).then_inc(x_in, 16)
            for w, src in enumerate((wq, wk, wv, wu, w_r, w_k, w_v)):
                sp.dma_start(probs[:, w // GH, w % GH, :].rearrange("p (o c) -> p o c", o=CB),
                             src.rearrange("(o p) c -> p o c", p=P)).then_inc(w_qk_in if w < 2 else w_in, 16)
            sp.dma_start(cos_sb[:, :], cos_t).then_inc(c_in, 16)
            sp.dma_start(sin_sb[:, :], sin_t).then_inc(c_in, 16)
            sp.dma_start(bu_sb[:, :], bu.rearrange("(a c) -> a c", a=1).to_broadcast([P, C])).then_inc(c_in, 16)
            for n, mu in enumerate((mu_r, mu_k)):
                for o in range(CB):
                    sp.dma_start(mu_sb[:, n, o:o + 1],
                                 mu[o * P:(o + 1) * P].rearrange("(p a) -> p a", a=1)).then_inc(c_in, 16)

            def carry_wait(b):
                if b.i is not None:
                    sp.sem_inc(sp_passed, 1)

            def step(b, par):
                def store_out():
                    s = b.plus(-2)
                    if s.active():
                        n = s.index(sp)
                        sp.wait_ge(out_done, s.count(2, 2))
                        carry_wait(b)
                        sp.dma_start(out[n].rearrange("(c p) d -> p c d", p=P),
                                     gate[:, :, :]).then_inc(out_stored, 16)

                def load_stacks(go):
                    s = b.plus(1)
                    if not s.active():
                        return
                    if go == 0:
                        sp.wait_ge(parts_out, s.count(32, 32))
                        carry_wait(b)
                        if b.plus(-1).has(SCORES, SCORES):
                            sp.wait_ge(st_ready, b.plus(-1).count(SCORES, SCORES))
                    n = 1 - par
                    q_src, k_src = scratch[n, 0], scratch[n, 1]
                    for part, copies, row in ((0, 3, 0),) if go == 0 else ((1, 2, 3 * D), (2, 1, 5 * D)):
                        rows = q_src[part * D:(part + 1) * D, :]
                        rep = bass.AP(rows.tensor, rows.offset, [[0, copies]] + [list(a) for a in rows.ap])
                        sp.dma_start(q_st[n][row:row + copies * D, :, :].rearrange("p h t -> p (h t)"),
                                     rep).then_inc(stack_in, 16)
                        sp.dma_start(k_st[n][row:row + copies * D, :, :].rearrange("p h t -> p (h t)"),
                                     k_src[0:copies * D, :]).then_inc(stack_in, 16)

                def move_attn(s, g):
                    if not s.active():
                        return
                    sp.wait_ge(attn_done, s.count(4, g + 1))
                    carry_wait(b)
                    if g == 0:
                        if s.plus(-1).has(2, 2):
                            sp.wait_ge(wu_ready, s.plus(-1).count(2, 2))
                    for j in range(GH):
                        row = (g * GH + j) * D
                        sp.dma_start(attnT[row % P:row % P + D, row // P, :],
                                     attn[32 * j:32 * j + D, :]).then_inc(attn_in, 16)

                def move_max(s, g):
                    if not s.active():
                        return
                    sp.wait_ge(msplit, s.count(16, 4 * g + 4))
                    dst = q_st[(s.add) % 2]
                    for m in range(MROWS):
                        sp.dma_start(dst[SROWS + m:SROWS + m + 1, g * GH:(g + 1) * GH, :]
                                     .rearrange("p h (c t) -> p (h c) t", c=TC),
                                     mparts[:, m, :]).then_inc(mrow_in, 16)

                def load_residual():
                    if b.active():
                        n = b.index(sp)
                        if b.plus(-2).has(2, 2):
                            sp.wait_ge(out_done, b.plus(-2).count(2, 2))
                        carry_wait(b)
                        sp.dma_start(y[par][:, :, :], x[n].rearrange("(c p) d -> p c d", p=P)).then_inc(xres_in, 16)

                def load_x():
                    s = b.plus(3)
                    if s.active():
                        n = s.index(sp)
                        sp.wait_ge(xT_ready, b.plus(2).count(2, 2))
                        carry_wait(b)
                        sp.dma_start(xn[:, :, :], x[n].rearrange("(c p) d -> p c d", p=P)).then_inc(x_in, 16)

                def store_parts(s, half, t):
                    if s.active():
                        sp.wait_ge(sub2, s.count(2, t + 1))
                        carry_wait(b)
                        if s.plus(-2).has(96, 96):
                            sp.wait_ge(stack_in, s.plus(-2).count(96, 96))
                        sp.dma_start(scratch[half, t].rearrange("(k r i) (h c) -> (i h) (k r) c", k=3, r=2, h=H),
                                     parts[:, t, :, :, :].rearrange("p k r c -> p (k r) c")).then_inc(parts_out, 16)

                move_attn(b.plus(-1), 3)
                move_max(b, 1)
                store_out()
                store_parts(b.plus(1), 1 - par, 1)
                load_stacks(0)
                load_x()
                load_residual()
                move_max(b, 2)
                load_stacks(1)
                move_attn(b, 0)
                move_max(b, 3)
                move_attn(b, 1)
                move_max(b.plus(1), 0)
                move_attn(b, 2)
                store_parts(b.plus(2), par, 0)

            steps(sp, step, FIRST + 1)
            sp.wait_ge(out_stored, 16 * B)

        @block.gpsimd
        def _(pool):
            nc.gpsimd.memset(ident[:, :], 0.0).then_inc(ident_ok, 1)
            pool.wait_ge(ident_ok, 1)
            nc.gpsimd.affine_select(out=ident[:, :], in_=ident[:, :], compare_op=ALU.not_equal, fill=1.0, base=0,
                                    pattern=[[-1, P]], channel_multiplier=1).then_inc(ident_ok, 1)
            pool.wait_ge(ident_ok, 2)
            nc.gpsimd.memset(mhalf[:, :], -0.5).then_inc(const_ok, 1)
            pool.wait_ge(const_ok, 1)

            def step(b, par):
                def finish():
                    s = b.plus(-2)
                    if s.active():
                        for n in range(2):
                            pool.wait_ge(gated, s.count(2, n + 1))
                            t = gate[:, 2 * n:2 * n + 2, :]
                            nc.gpsimd.tensor_tensor(t, t, y[par][:, 2 * n:2 * n + 2, :], ALU.add).then_inc(out_done, 1)

                def add_bu():
                    s = b.plus(-1)
                    if s.active():
                        pool.wait_ge(xres_in, s.count(16, 16))
                        nc.gpsimd.tensor_tensor(y[1 - par][:, :, :], y[1 - par][:, :, :],
                                                bu_sb[:, :].rearrange("p (a c) -> p a c", a=1)
                                                .to_broadcast([P, TC, C]), ALU.add).then_inc(bu_added, 1)

                def rope_mults(t, r):
                    s = b.plus(2)
                    if s.active() and not first(s):
                        k = 6 * t + 2 * r
                        pool.wait_ge(qk_done, s.count(4, 2 * t + r + 1))
                        if r == 0:
                            if s.plus(-1).has(2, t + 1):
                                pool.wait_ge(sub2, s.plus(-1).count(2, t + 1))
                            nc.gpsimd.tensor_tensor(rot[:, t, 1, :], rope_t[:, 0, :], sin_sb[:, :],
                                                    ALU.mult).then_inc(rope_step, 1)
                            nc.gpsimd.tensor_tensor(rot[:, t, 0, :], rope_t[:, 0, :], cos_sb[:, :],
                                                    ALU.mult).then_inc(rope_step, 1)
                        else:
                            pool.wait_ge(rope_step, s.count(12, k))
                            nc.gpsimd.tensor_tensor(rope_t[:, 0, :], rope_t[:, 1, :], cos_sb[:, :],
                                                    ALU.mult).then_inc(rope_step, 1)
                            pool.wait_ge(rope_step, s.count(12, k + 1))
                            nc.gpsimd.tensor_tensor(rope_t[:, 1, :], rope_t[:, 1, :], sin_sb[:, :],
                                                    ALU.mult).then_inc(rope_step, 1)

                def rope_sums(t):
                    s = b.plus(2)
                    if s.active() and not first(s):
                        pool.wait_ge(rope_step, s.count(12, 6 * t + 3))
                        nc.gpsimd.tensor_tensor(rot[:, t, 1, :], rot[:, t, 1, :], rope_t[:, 0, :],
                                                ALU.add).then_inc(rope_step, 1)
                        pool.wait_ge(rope_step, s.count(12, 6 * t + 4))
                        nc.gpsimd.tensor_tensor(rot[:, t, 0, :], rot[:, t, 0, :], rope_t[:, 1, :],
                                                ALU.subtract).then_inc(rope_step, 1)

                def rest1(t):
                    s = b.plus(2)
                    if s.active() and not first(s):
                        pool.wait_ge(hi_done, s.count(2, t + 1))
                        nc.gpsimd.tensor_tensor(rot[:, t, :, :], rot[:, t, :, :], parts[:, t, 0, :, :],
                                                ALU.subtract).then_inc(sub1, 1)

                def rest2(s, t):
                    if s.active() and not first(s):
                        pool.wait_ge(lo_done, s.count(2, t + 1))
                        nc.gpsimd.tensor_tensor(parts[:, t, 2, :, :], rot[:, t, :, :], parts[:, t, 1, :, :],
                                                ALU.subtract).then_inc(sub2, 1)

                def difference(o):
                    s = b.plus(-1)
                    if s.active():
                        pool.wait_ge(ynT_done, s.count(2, o + 1))
                        if s.plus(-1).has(2, o + 1):
                            pool.wait_ge(r_lo_done, s.plus(-1).count(2, o + 1))
                        nc.gpsimd.tensor_tensor(xrT[:, o, :], ynT[:, o, 1:T + 1], ynT[:, o, 0:T],
                                                ALU.subtract).then_inc(diff_done, 1)

                def low_r(o):
                    s = b.plus(-1)
                    if s.active():
                        pool.wait_ge(r_hi_done, s.count(2, o + 1))
                        nc.gpsimd.tensor_tensor(r_lo[:, o, :], xrT[:, o, :], r_hi[:, o, :],
                                                ALU.subtract).then_inc(r_lo_done, 1)

                def low_a(o):
                    s = b.plus(-1)
                    if s.active():
                        pool.wait_ge(a_hi_done, s.count(2, o + 1))
                        nc.gpsimd.tensor_tensor(f_lo[:, o, :], attnT[:, o, :], f_hi[:, o, :],
                                                ALU.subtract).then_inc(a_lo_done, 1)

                def low_f(k, o):
                    s = b.plus(-1)
                    if s.active():
                        pool.wait_ge(f_hi_done, s.count(4, 2 * k + o + 1))
                        nc.gpsimd.tensor_tensor(f_lo[:, o, :], mixT[:, o, :], f_hi[:, o, :],
                                                ALU.subtract).then_inc(f_lo_done, 1)

                def scales(s, n, stat, scale, ve, mean, rs, nm):
                    if s.active():
                        a, z = 2 * n, 2 * n + 2
                        pool.wait_ge(stat, s.count(6, 3 * n + 3))
                        nc.gpsimd.tensor_tensor(rs[:, a:z], ve[:, a:z], mhalf[:, :], ALU.pow).then_inc(scale, 1)
                        pool.wait_ge(scale, s.count(4, 2 * n + 1))
                        nc.gpsimd.tensor_tensor(nm[:, a:z], mean[:, a:z], rs[:, a:z], ALU.mult).then_inc(scale, 1)

                def square(o):
                    s = b.plus(-1)
                    if s.active():
                        pool.wait_ge(relu_done, s.count(2, o + 1))
                        nc.gpsimd.tensor_tensor(mixT[:, o, :], mixT[:, o, :], mixT[:, o, :], ALU.mult).then_inc(ksq_done, 1)

                finish()
                add_bu()
                low_a(0)
                rest2(b.plus(1), 1)
                low_a(1)
                for n in range(2):
                    scales(b.plus(-1), n, ln2_stat, ln2_scale, ve2, mean2, rs2, nm2)
                rope_mults(0, 0)
                rope_mults(0, 1)
                rope_sums(0)
                difference(0)
                difference(1)
                low_f(0, 0)
                low_f(0, 1)
                rope_mults(1, 0)
                low_r(0)
                rope_mults(1, 1)
                square(0)
                low_r(1)
                scales(b.plus(3), 0, ln1_stat, ln1_scale, ve1, mean1, rs1, nm1)
                rest1(0)
                square(1)
                low_f(1, 0)
                low_f(1, 1)
                scales(b.plus(3), 1, ln1_stat, ln1_scale, ve1, mean1, rs1, nm1)
                rope_sums(1)
                rest2(b.plus(2), 0)
                rest1(1)

            step(Seq(FIRST), FIRST % 2)
            for n in range(2):
                pool.wait_ge(const_ok, 2 * n + 1)
                nc.gpsimd.memset(v_ext[n][:, :, :], 1.0).then_inc(const_ok, 1)
                pool.wait_ge(const_ok, 2 * n + 2)
                nc.gpsimd.memset(k_st[n][SROWS:SROWS + MROWS, :, :], 1.0).then_inc(const_ok, 1)
            pool.wait_ge(const_ok, 5)
            nc.gpsimd.memset(ynT[:, :, 0:1], 0.0).then_inc(const_ok, 1)
            pool.wait_ge(const_ok, 6)
            pool.wait_ge(c_in, 16 * CONSTS)
            steps(pool, step, FIRST + 1)

        @block.scalar
        def _(act):
            def step(b, par):
                def v_evac(n):
                    s = b.plus(1)
                    if s.active():
                        act.wait_ge(v_ready, s.count(2, n + 1))
                        if b.plus(-1).has(UNITS, UNITS):
                            act.wait_ge(pv_done, b.plus(-1).count(UNITS, UNITS))
                        nc.scalar.activation(
                            v_ext[1 - par][:, 2 * n:2 * n + 2, 0:H * VW].rearrange("p c (h d) -> p c h d", h=H)[:, :, :, 0:D],
                            d_ps[:, BANK["V", n], :].rearrange("p (c h d) -> p c h d", c=2, h=H), ACT.Copy).then_inc(v_done, 1)

                def xT_evac(n):
                    s = b.plus(2)
                    if s.active():
                        act.wait_ge(xT_ready, s.count(2, n + 1))
                        if s.plus(-1).has(2, 2):
                            act.wait_ge(v_ready, s.plus(-1).count(2, 2))
                        nc.scalar.activation(xnT_hi[:, n, :], d_ps[:, BANK["XT", n], :], ACT.Copy).then_inc(xnT_done, 1)

                def yT_evac(n):
                    s = b.plus(-1)
                    if s.active():
                        act.wait_ge(yT_ready, s.count(2, n + 1))
                        if s.plus(-1).has(4, 4):
                            act.wait_ge(shift_done, s.plus(-1).count(4, 4))
                        if b.has(NG, 1):
                            act.wait_ge(attn_done, b.count(NG, 1))
                        nc.scalar.activation(ynT[:, n, 1:T + 1], d_ps[:, BANK["YT", n], :], ACT.Copy).then_inc(ynT_done, 1)

                def norm1(c):
                    s = b.plus(2)
                    if s.active():
                        act.wait_ge(ln1_scale, s.count(4, 2 * (c // 2) + 2))
                        nc.scalar.activation(xn[:, c, :], xn[:, c, :], ACT.Identity, scale=rs1[:, c:c + 1],
                                             bias=nm1[:, c:c + 1]).then_inc(xn_done, 1)

                def norm2(n):
                    s = b.plus(-1)
                    if s.active():
                        act.wait_ge(ln2_scale, s.count(4, 2 * n + 2))
                        if s.plus(-1).has(4, 4):
                            act.wait_ge(f_lo_done, s.plus(-1).count(4, 4))
                        for c in (2 * n, 2 * n + 1):
                            nc.scalar.activation(yn[:, c, :], y[1 - par][:, c, :], ACT.Identity, scale=rs2[:, c:c + 1],
                                                 bias=nm2[:, c:c + 1]).then_inc(yn_done, 1)

                def qk_evac(t, r):
                    s = b.plus(2)
                    if s.active():
                        act.wait_ge(qk_ready, s.count(4, 2 * t + r + 1))
                        if s.has(12, 6 * t):
                            act.wait_ge(rope_step, s.count(12, 6 * t))
                        nc.scalar.activation(rope_t[:, r, :], d_ps[:, BANK["QK"[t], r], :],
                                             ACT.Copy).then_inc(qk_done, 1)

                def high(t):
                    s = b.plus(2)
                    if s.active():
                        act.wait_ge(rope_step, s.count(12, 6 * t + 6))
                        if s.plus(-1).has(32, 32):
                            act.wait_ge(parts_out, s.plus(-1).count(32, 32))
                        nc.scalar.activation(parts[:, t, 0, :, :], rot[:, t, :, :], ACT.Copy).then_inc(hi_done, 1)

                def middle(s, t):
                    if s.active():
                        act.wait_ge(sub1, s.count(2, t + 1))
                        nc.scalar.activation(parts[:, t, 1, :, :], rot[:, t, :, :], ACT.Copy).then_inc(lo_done, 1)

                def relu(n):
                    s = b.plus(-1)
                    if s.active():
                        act.wait_ge(k_ready, s.count(2, n + 1))
                        act.wait_ge(f_lo_done, s.count(4, n + 1))
                        nc.scalar.activation(mixT[:, n, :], d_ps[:, BANK["FK", n], :], ACT.Relu).then_inc(relu_done, 1)

                def high_r(o):
                    s = b.plus(-1)
                    if s.active():
                        act.wait_ge(shift_done, s.count(4, 3 + o))
                        if s.plus(-1).has(2, 2):
                            act.wait_ge(r_ready, s.plus(-1).count(2, 2))
                        nc.scalar.activation(r_hi[:, o, :], xrT[:, o, :], ACT.Copy).then_inc(r_hi_done, 1)

                def high_a(o):
                    s = b.plus(-1)
                    if s.active():
                        act.wait_ge(attn_in, s.count(64 * NG, 64 * 2 * (o + 1)))
                        if s.plus(-1).has(2, 2):
                            act.wait_ge(o_ready, s.plus(-1).count(2, 2))
                        nc.scalar.activation(f_hi[:, o, :], attnT[:, o, :], ACT.Copy).then_inc(a_hi_done, 1)

                def high_f(k, o):
                    s = b.plus(-1)
                    if not s.active():
                        return
                    if k == 0:
                        act.wait_ge(shift_done, s.count(4, 1 + o))
                        act.wait_ge(wu_ready, s.count(2, 2))
                    else:
                        act.wait_ge(ksq_done, s.count(2, o + 1))
                        act.wait_ge(k_ready, s.count(2, 2))
                    nc.scalar.activation(f_hi[:, o, :], mixT[:, o, :], ACT.Copy).then_inc(f_hi_done, 1)

                def tanh(n):
                    s = b.plus(-1)
                    if s.active():
                        act.wait_ge(r_ready, s.count(2, n + 1))
                        if s.has(16, 0):
                            act.wait_ge(out_stored, s.count(16, 0))
                        nc.scalar.activation(gate[:, 2 * n:2 * n + 2, :].rearrange("p c d -> p (c d)"),
                                             d_ps[:, BANK["R", n], :], ACT.Tanh, scale=0.5).then_inc(tanh_done, 1)

                extras = {(0, 0): [(norm1, 0)], (0, 2): [(norm1, 1)], (1, 0): [(middle, b.plus(1), 1)],
                          (1, 2): [(high_a, 0)], (1, 3): [(v_evac, 0)],
                          (2, 0): [(norm1, 2)], (2, 1): [(norm1, 3)], (2, 3): [(v_evac, 1)],
                          (3, 1): [(high_a, 1)], (3, 2): [(xT_evac, 0)], (3, 3): [(xT_evac, 1)],
                          (6, 0): [(norm2, 0)], (6, 3): [(qk_evac, 0, 0)],
                          (7, 2): [(norm2, 1)], (7, 3): [(qk_evac, 0, 1)], (8, 2): [(yT_evac, 0)],
                          (8, 3): [(yT_evac, 1)], (9, 3): [(qk_evac, 1, 0)], (10, 0): [(high_f, 0, 0)],
                          (10, 1): [(high_f, 0, 1)], (11, 1): [(high, 0)], (10, 3): [(qk_evac, 1, 1)],
                          (11, 0): [(high_r, 0)], (11, 3): [(relu, 0)], (12, 0): [(high_r, 1)],
                          (12, 3): [(relu, 1)], (13, 1): [(high_f, 1, 0)], (13, 3): [(tanh, 0)],
                          (14, 0): [(high_f, 1, 1)], (14, 3): [(tanh, 1)],
                          (15, 0): [(middle, b.plus(2), 0)], (15, 2): [(high, 1)]}
                if first(b.plus(2)):
                    extras[15, 3] = [(middle, b.plus(2), 1)]
                elif first(b.plus(1)):
                    del extras[1, 0]
                for u in range(UNITS):
                    for j in range(GH):
                        if b.active():
                            n = GH * u + j
                            act.wait_ge(st_ready, b.count(SCORES, n + 1))
                            if j == 0:
                                if b.has(UNITS, u - SLOTS + 1):
                                    act.wait_ge(pv_done, b.count(UNITS, u - SLOTS + 1))
                            nc.scalar.activation(probs[:, u % SLOTS, j, :], st_ps[:, n % 2, :], ACT.Exp,
                                                 scale=float(D) ** -0.5).then_inc(exp_done, 1)
                        for f, *args in extras.get((u, j), []):
                            f(*args)

            steps(act, step)

        @block.vector
        def _(dve):
            def turned_weight(w, name):
                dve.wait_ge(wT_ready, w + 1)
                src = weight_bank(w).rearrange("p (o i c) -> p o i c", o=CB, i=CB)
                scale = 0.5 if name == "fv" else 1.0

                def places(tile):
                    for o in range(CB):
                        for i in range(CB):
                            if name in ("q", "k"):
                                yield (src[:, o, i, :].rearrange("p (h i r) -> p r i h", i=HALF, r=2),
                                       tile[:, i, :].rearrange("p (r i h) -> p r i h", r=2, h=H)[:, :, :, o * 8:o * 8 + 8])
                            else:
                                yield src[:, o, i, :], tile[:, i, o * P:(o + 1) * P]

                for block, dst in places(w_hi[name]):
                    nc.vector.tensor_scalar(dst, block, scale, None, ALU.mult).then_inc(w_hi_done, 1)
                dve.wait_ge(w_hi_done, 4 * w + 4)
                for (block, dst), (_, high) in zip(places(w_lo[name]), places(w_hi[name])):
                    for r in range(2) if name in ("q", "k") else (slice(None),):
                        ins = nc.vector.scalar_tensor_tensor(out=dst[:, r], in0=block[:, r], scalar=scale,
                                                             in1=high[:, r], op0=ALU.mult, op1=ALU.subtract)
                ins.then_inc(wT_done, 1)

            def step(b, par):
                def row_max(u, qc):
                    s, h = row_max_at(b, u)
                    if s.active():
                        n = h * TC + qc
                        dve.wait_ge(s_ready, s.count(SCORES, n + 1))
                        nc.vector.tensor_reduce(mx[:, n:n + 1], s_ps[:, n % 2, :], AX.X, ALU.max).then_inc(max_done, 1)

                def split_max(s, g, half):
                    if not s.active():
                        return
                    m = d_ps[0:GH * TC, BANK["M", g], 0:P]
                    if half == 0:
                        dve.wait_ge(mt_ready, s.count(4, g + 1))
                        if s.has(48 * NG, 48 * g):
                            dve.wait_ge(mrow_in, s.count(48 * NG, 48 * g))
                        nc.vector.tensor_scalar(mparts[:, 0, :], m, -1.0, None, ALU.mult).then_inc(msplit, 1)
                        dve.wait_ge(msplit, s.count(16, 4 * g + 1))
                        nc.vector.scalar_tensor_tensor(out=mres[:, :], in0=m, scalar=-1.0, in1=mparts[:, 0, :],
                                                       op0=ALU.mult, op1=ALU.subtract).then_inc(msplit, 1)
                    else:
                        dve.wait_ge(msplit, s.count(16, 4 * g + 2))
                        nc.vector.tensor_copy(mparts[:, 1, :], mres[:, :]).then_inc(msplit, 1)
                        dve.wait_ge(msplit, s.count(16, 4 * g + 3))
                        nc.vector.tensor_tensor(mparts[:, 2, :], mres[:, :], mparts[:, 1, :],
                                                ALU.subtract).then_inc(msplit, 1)

                def normalise(s, g, stage):
                    if not s.active():
                        return
                    blocks = sums.rearrange("p (k r) -> p k r", r=32)
                    if stage == 0:
                        dve.wait_ge(pv_done, s.count(UNITS, TC * (g + 1)))
                        if s.has(NG, g):
                            dve.wait_ge(attn_done, s.count(NG, g))
                        if g == 1 and s.plus(-1).has(4, 4):
                            dve.wait_ge(shift_done, s.plus(-1).count(4, 4))
                        nc.vector.transpose(sums, pv_ps[:, g % 2, :]).then_inc(norm_step, 1)
                    elif stage == 1:
                        dve.wait_ge(norm_step, s.count(3 * NG, 3 * g + 1))
                        nc.vector.reciprocal(inv[:, :], blocks[:, :, D]).then_inc(norm_step, 1)
                        dve.wait_ge(norm_step, s.count(3 * NG, 3 * g + 2))
                        nc.vector.tensor_tensor(blocks[:, :, 0:D], blocks[:, :, 0:D],
                                                inv[:, :].rearrange("p (k r) -> p k r", r=1)
                                                .to_broadcast([P, T // 32, D]), ALU.mult).then_inc(norm_step, 1)
                    else:
                        dve.wait_ge(norm_step, s.count(3 * NG, 3 * g + 3))
                        if s.has(64 * NG, 64 * g):
                            dve.wait_ge(attn_in, s.count(64 * NG, 64 * g))
                        nc.vector.transpose(attn[:, :], sums).then_inc(attn_done, 1)

                def residual(n):
                    s = b.plus(-1)
                    if not s.active():
                        return
                    if n == 0:
                        dve.wait_ge(bu_added, s.count(1, 1))
                    dve.wait_ge(wu_ready, s.count(2, n + 1))
                    t = y[1 - par][:, 2 * n:2 * n + 2, :].rearrange("p c d -> p (c d)")
                    nc.vector.tensor_tensor(t, d_ps[:, BANK["WU", n], :], t, ALU.add).then_inc(res_done, 1)

                def layer_stats(s, n, stage, done, src, stats, mv, ve, nm, used):
                    a, z = 2 * n, 2 * n + 2
                    chunks, per, k = range(a, z), 6, 3 * n
                    if stage == 0:
                        for c in chunks:
                            ins = nc.vector.bn_stats(stats[:, c, :], src[:, c, :])
                        ins.then_inc(done, 1)
                        return
                    dve.wait_ge(done, s.count(per, k + 1))
                    dve.sem_inc(dve_passed, 1)
                    for c in chunks:
                        ins = nc.vector.bn_aggr(mv[:, c, :], stats[:, c, :])
                    ins.then_inc(done, 1)
                    dve.wait_ge(done, s.count(per, k + 2))
                    if s.plus(-1).has(4, 4):
                        dve.wait_ge(used, s.plus(-1).count(4, 4))
                    nc.vector.tensor_scalar(ve[:, a:z], mv[:, a:z, 1], EPS, None, ALU.add)
                    nc.vector.tensor_scalar(nm[:, a:z], mv[:, a:z, 0], -1.0, None, ALU.mult).then_inc(done, 1)

                def stats1_of(n, stage):
                    s = b.plus(3)
                    if s.active():
                        if stage == 0:
                            dve.wait_ge(x_in, s.count(16, 16))
                        layer_stats(s, n, stage, ln1_stat, xn, stats1, mv1, ve1, mean1, xn_done)

                def stats2_of(n, stage):
                    s = b.plus(-1)
                    if s.active():
                        if stage == 0:
                            dve.wait_ge(res_done, s.count(2, n + 1))
                        layer_stats(s, n, stage, ln2_stat, y[1 - par], stats2, mv2, ve2, mean2, yn_done)

                def split_xnT(n):
                    s = b.plus(2)
                    if s.active():
                        dve.wait_ge(xnT_done, s.count(2, n + 1))
                        nc.vector.tensor_tensor(xnT_lo[:, n, :], d_ps[:, BANK["XT", n], :], xnT_hi[:, n, :],
                                                ALU.subtract).then_inc(xnT_split, 1)

                def shift(n, o):
                    s = b.plus(-1)
                    if not s.active():
                        return
                    if n == 1:
                        dve.wait_ge(diff_done, s.count(2, o + 1))
                        dve.wait_ge(yT_ready, s.count(2, 2))
                    dst = (xrT, mixT)[n]
                    nc.vector.scalar_tensor_tensor(out=dst[:, o, :], in0=xrT[:, o, :], in1=ynT[:, o, 0:T],
                                                   scalar=mu_sb[:, n, o:o + 1], op0=ALU.mult,
                                                   op1=ALU.add).then_inc(shift_done, 1)

                def gate_v(s, n):
                    if s.active():
                        dve.wait_ge(o_ready, s.count(2, n + 1))
                        dve.wait_ge(tanh_done, s.count(2, n + 1))
                        t = gate[:, 2 * n:2 * n + 2, :].rearrange("p c d -> p (c d)")
                        nc.vector.scalar_tensor_tensor(out=t, in0=t, scalar=1.0, in1=d_ps[:, BANK["O", n], :],
                                                       op0=ALU.add, op1=ALU.mult).then_inc(gated, 1)

                def first_rope(t):
                    if not first(b.plus(2)):
                        return
                    k = 6 * t
                    dve.wait_ge(qk_done, 2 * t + 1)
                    nc.vector.tensor_tensor(rot[:, t, 1, :], rope_t[:, 0, :], sin_sb[:, :], ALU.mult).then_inc(rope_step, 1)
                    nc.vector.tensor_tensor(rot[:, t, 0, :], rope_t[:, 0, :], cos_sb[:, :], ALU.mult).then_inc(rope_step, 1)
                    dve.wait_ge(rope_step, k + 2)
                    dve.wait_ge(qk_done, 2 * t + 2)
                    nc.vector.tensor_tensor(rope_t[:, 0, :], rope_t[:, 1, :], cos_sb[:, :], ALU.mult).then_inc(rope_step, 1)
                    dve.wait_ge(rope_step, k + 3)
                    nc.vector.tensor_tensor(rope_t[:, 1, :], rope_t[:, 1, :], sin_sb[:, :], ALU.mult).then_inc(rope_step, 1)
                    nc.vector.tensor_tensor(rot[:, t, 1, :], rot[:, t, 1, :], rope_t[:, 0, :], ALU.add).then_inc(rope_step, 1)
                    dve.wait_ge(rope_step, k + 4)
                    nc.vector.tensor_tensor(rot[:, t, 0, :], rot[:, t, 0, :], rope_t[:, 1, :],
                                            ALU.subtract).then_inc(rope_step, 1)

                def first_rest(t, part):
                    if not first(b.plus(2)):
                        return
                    if part == 0:
                        dve.wait_ge(hi_done, t + 1)
                        nc.vector.tensor_tensor(rot[:, t, :, :], rot[:, t, :, :], parts[:, t, 0, :, :],
                                                ALU.subtract).then_inc(sub1, 1)
                    else:
                        dve.wait_ge(lo_done, t + 1)
                        nc.vector.tensor_tensor(parts[:, t, 2, :, :], rot[:, t, :, :], parts[:, t, 1, :, :],
                                                ALU.subtract).then_inc(sub2, 1)

                prev, nxt = b.plus(-1), b.plus(1)
                extras = {(0, 0): [(gate_v, b.plus(-2), 0)], (0, 3): [(gate_v, b.plus(-2), 1)],
                          (1, 0): [(normalise, prev, 3, 0)], (1, 1): [(normalise, prev, 3, 1)],
                          (1, 3): [(normalise, prev, 3, 2)],
                          (2, 1): [(split_max, b, 1, 0)], (2, 2): [(split_max, b, 1, 1)],
                          (3, 3): [(split_xnT, 0)], (4, 0): [(split_xnT, 1)], (4, 3): [(residual, 0)],
                          (5, 0): [(stats2_of, 0, 0)], (5, 1): [(stats2_of, 0, 1)], (5, 3): [(residual, 1)],
                          (6, 0): [(split_max, b, 2, 0)], (6, 1): [(split_max, b, 2, 1)],
                          (6, 2): [(stats2_of, 1, 0)], (6, 3): [(stats2_of, 1, 1)],
                          (7, 0): [(normalise, b, 0, 0)], (7, 1): [(normalise, b, 0, 1)],
                          (7, 3): [(normalise, b, 0, 2)],
                          (8, 3): [(stats1_of, 0, 0)], (9, 1): [(stats1_of, 0, 1)],
                          (9, 3): [(shift, 1, 0), (shift, 1, 1)],
                          (10, 1): [(split_max, b, 3, 0)], (10, 2): [(split_max, b, 3, 1)],
                          (10, 3): [(shift, 0, 0)], (11, 2): [(shift, 0, 1)],
                          (12, 0): [(normalise, b, 1, 0)], (12, 1): [(normalise, b, 1, 1)],
                          (12, 3): [(normalise, b, 1, 2)],
                          (13, 3): [(stats1_of, 1, 0)], (14, 0): [(stats1_of, 1, 1)],
                          (14, 1): [(split_max, nxt, 0, 0)], (14, 2): [(split_max, nxt, 0, 1)],
                          (15, 0): [(normalise, b, 2, 0)], (15, 1): [(normalise, b, 2, 1)],
                          (15, 3): [(normalise, b, 2, 2)]}
                if first(b.plus(2)):
                    extras[5, 0] = [(first_rope, 0), (first_rope, 1), (first_rest, 0, 0)]
                    extras[7, 3] = extras.pop((8, 3)) + extras.pop((9, 1)) + extras.pop((13, 3)) + extras.pop((14, 0))
                    extras[8, 0] = [(first_rest, 0, 1), (first_rest, 1, 0), (first_rest, 1, 1)]
                for u in range(UNITS):
                    for qc in range(TC):
                        row_max(u, qc)
                        for f, *args in extras.get((u, qc), []):
                            f(*args)

            step(Seq(FIRST), FIRST % 2)
            for w in range(4):
                turned_weight(w, WEIGHTS[w])
            dve.wait_ge(c_in, 16 * CONSTS)
            step(Seq(FIRST + 1), (FIRST + 1) % 2)
            for w in range(4, 7):
                turned_weight(w, WEIGHTS[w])
            steps(dve, step, FIRST + 2)

        @block.tensor
        def _(pe):
            pe.wait_ge(ident_ok, 2)
            pe.wait_ge(w_qk_in, 16 * 2)
            for w in range(7):
                if w == 2:
                    pe.wait_ge(w_in, 16 * 5)
                src = probs[:, w // GH, w % GH, :].rearrange("p (o c) -> p o c", o=CB)
                for o in range(CB):
                    for i in range(CB):
                        ins = nc.tensor.transpose(weight_bank(w)[:, (o * CB + i) * P:(o * CB + i + 1) * P],
                                                  src[:, o, i * P:(i + 1) * P], ident[:, :])
                ins.then_inc(wT_ready, 1)
            pe.wait_ge(wT_done, 2)

            def step(b, par):
                def score_T(u, j):
                    if not b.active():
                        return
                    g, c = divmod(u, TC)
                    n, h = GH * u + j, GH * g + j
                    if c == 0 and j == 0:
                        pe.wait_ge(mrow_in, b.count(48 * NG, 48 * (g + 1)))
                    if b.has(SCORES, n - 1):
                        pe.wait_ge(exp_done, b.count(SCORES, n - 1))
                    nc.tensor.matmul(st_ps[:, n % 2, :], k_st[par][0:SROWS + MROWS, h, c * P:(c + 1) * P],
                                     q_st[par][0:SROWS + MROWS, h, :], start=True, stop=True).then_inc(st_ready, 1)

                def score(u, qc):
                    s, h = row_max_at(b, u)
                    if not s.active():
                        return
                    n, half = h * TC + qc, s.add % 2
                    if n == 0:
                        pe.wait_ge(stack_in, s.count(96, 96))
                        if first(s):
                            pe.wait_ge(wT_done, 7)
                    if s.has(SCORES, n - 1):
                        pe.wait_ge(max_done, s.count(SCORES, n - 1))
                    nc.tensor.matmul(s_ps[:, n % 2, :], q_st[half][0:SROWS, h, qc * P:(qc + 1) * P],
                                     k_st[half][0:SROWS, h, :], start=True, stop=True).then_inc(s_ready, 1)

                def values(s, half, u):
                    if not s.active():
                        return
                    g, c = divmod(u, TC)
                    pe.wait_ge(exp_done, s.count(SCORES, GH * (u + 1)))
                    if u == 0:
                        pe.wait_ge(v_done, s.count(2, 2))
                    if c == 0 and s.has(3 * NG, 3 * g - 5):
                        pe.wait_ge(norm_step, s.count(3 * NG, 3 * g - 5))
                    for j in range(GH):
                        h = GH * g + j
                        ins = nc.tensor.matmul(pv_ps[32 * j:32 * j + 32, g % 2, :], v_ext[half][:, c, VW * h:VW * h + 32],
                                               probs[:, u % SLOTS, j, :], start=(c == 0), stop=(c == TC - 1))
                    ins.then_inc(pv_done, 1)

                def open_bank(name, n):
                    free = bank_reader(b, NUMBER[name, n])
                    if free is not None:
                        pe.wait_ge(free[0], free[1])
                    return d_ps[:, BANK[name, n], :]

                def row_max_T(s, g):
                    if not s.active():
                        return
                    pe.wait_ge(max_done, s.count(SCORES, GH * TC * (g + 1)))
                    w = GH * TC
                    bank = open_bank("M", g)
                    nc.tensor.transpose(bank[0:w, 0:P], mx[:, g * w:(g + 1) * w], ident[:, :]).then_inc(mt_ready, 1)

                def turn(s, name, n, src, src_done, done):
                    if not s.active():
                        return
                    bank = open_bank(name, n)
                    pe.wait_ge(src_done, s.count(4, 4))
                    for c in range(TC):
                        ins = nc.tensor.transpose(bank[:, c * P:(c + 1) * P], src[:, c, n * P:(n + 1) * P], ident[:, :])
                    ins.then_inc(done, 1)

                def products(bank, w, x, first, last):
                    for k, (a, z) in enumerate(((0, 0), (0, 1), (1, 0))):
                        ins = nc.tensor.matmul(bank, w[a], x[z], start=first and k == 0, stop=last and k == 2)
                    return ins

                def channel_rows(s, name, n, i, w, src, src_done, per, k, done):
                    if not s.active():
                        return
                    bank = open_bank(name, n) if i == 0 else d_ps[:, BANK[name, n], :]
                    if i == 0:
                        pe.wait_ge(src_done, s.count(per, k))
                    ins = products(bank, [t[:, i, n * P:(n + 1) * P] for t in w], [t[:, i, :] for t in src],
                                   i == 0, i == CB - 1)
                    if i == CB - 1:
                        ins.then_inc(done, 1)

                def token_rows(s, name, n, m, w, src, src_done, per, k, done):
                    if not s.active():
                        return
                    bank = open_bank(name, n) if m == 0 else d_ps[:, BANK[name, n], :]
                    if m == 0:
                        pe.wait_ge(src_done, s.count(per, k))
                    c = 2 * n + m
                    for i in range(CB):
                        out_half = bank[:, m * C:(m + 1) * C]
                        ins = products(out_half, [t[:, i, c * P:(c + 1) * P] for t in src],
                                       [t[:, i, :] for t in w], i == 0, i == CB - 1)
                    if m == 1:
                        ins.then_inc(done, 1)

                def weight(name):
                    return w_hi[name], w_lo[name]

                def dense(u, half):
                    name = DENSE[u]
                    prev = b.plus(-1)
                    if name == "XT":
                        turn(b.plus(2), "XT", half, xn, xn_done, xT_ready)
                    elif name == "YT":
                        turn(prev, "YT", half, yn, yn_done, yT_ready)
                    elif name[:-1] in ("Q", "K"):
                        channel_rows(b.plus(2), name[0], int(name[1]), half,
                                     weight(name[0].lower()), (xnT_hi, xnT_lo), xnT_split, 2, 2, qk_ready)
                    elif name[:-1] == "FK":
                        channel_rows(prev, "FK", int(name[-1]), half, weight("fk"), (f_hi, f_lo), f_lo_done, 4, 2, k_ready)
                    elif name[:-1] == "V":
                        token_rows(b.plus(1), "V", int(name[-1]), half, weight("v"), (xnT_hi, xnT_lo),
                                   xnT_split, 2, 2, v_ready)
                    elif name[:-1] == "WU":
                        token_rows(prev, "WU", int(name[-1]), half, weight("u"), (f_hi, f_lo), a_lo_done, 2, 2, wu_ready)
                    elif name[:-1] == "R":
                        token_rows(prev, "R", int(name[-1]), half, weight("r"), (r_hi, r_lo), r_lo_done, 2, 2, r_ready)
                    elif name[:-1] == "O":
                        token_rows(b.plus(-2) if name == "O1" else prev, "O", int(name[-1]), half, weight("fv"), (f_hi, f_lo), f_lo_done, 4, 4, o_ready)

                for u in range(UNITS):
                    for j in range(GH):
                        score_T(u, j)
                        score(u, j)
                        if j in (1, 2):
                            dense(u, j - 1)
                    if u == 0:
                        values(b.plus(-1), 1 - par, UNITS - 1)
                    else:
                        values(b, par, u - 1)
                    if u in MAX_T:
                        d, g = MAX_T[u]
                        row_max_T(b.plus(d), g)

            for b in range(FIRST, -1):
                step(Seq(b), b % 2)
            pe.wait_ge(wT_done, 4)
            pe.wait_ge(const_ok, 6)
            steps(pe, step, -1)


_INS = ["L0_attn_x", "L0_attn_Wq", "L0_attn_Wk", "L0_attn_Wv", "L0_attn_Wu", "L0_attn_bu",
        "L0_ffn_W_r", "L0_ffn_W_k", "L0_ffn_W_v", "L0_ffn_mu_r", "L0_ffn_mu_k"]


def kernel(**inputs):
    import numpy as np
    import concourse.bacc as bacc
    from concourse.bass_utils import run_bass_kernel_spmd

    half = C // 2
    theta = (np.float32(1.0) / np.float32(10000.0) ** (np.arange(half, dtype=np.float32) / np.float32(half))).astype(np.float32)
    angle = np.arange(T, dtype=np.float32)[None, :] * theta[:, None]
    order = np.arange(half).reshape(H, HALF).T.reshape(-1)
    tables = {"cos": np.cos(angle)[order].astype(np.float32), "sin": np.sin(angle)[order].astype(np.float32)}

    nc = bacc.Bacc("TRN2", target_bir_lowering=False, num_devices=1)
    arrays, args = {}, []
    for name, a in [(n, inputs[n]) for n in _INS] + list(tables.items()):
        a = np.ascontiguousarray(a)
        arrays[f"in_{name}_dram"] = a
        args.append(nc.dram_tensor(f"in_{name}_dram", a.shape, mybir.dt.from_np(a.dtype), kind="ExternalInput").ap())
    args.append(nc.dram_tensor("out_0_dram", (B, T, C), F32, kind="ExternalOutput").ap())
    layer_kernel(nc, *args)
    r = run_bass_kernel_spmd(nc, [arrays], core_ids=[0])
    return r.results[0]["out_0_dram"]
```
